# Optimizing a Trainium2 kernel written in Bass

```python
import numpy as np
import jax
import jax.numpy as jnp

def _softmax(x, axis=-1):
    return jax.nn.softmax(x, axis=axis)

def _gelu(x):
    return jax.nn.gelu(x, approximate=True)

def _silu(x):
    return jax.nn.silu(x)

def _sigmoid(x):
    return jax.nn.sigmoid(x)

def _layernorm(x, axis=-1, eps=1e-05):
    m = jnp.mean(x, axis=axis, keepdims=True)
    v = jnp.var(x, axis=axis, keepdims=True)
    return (x - m) / jnp.sqrt(v + eps)

def _scatter_add(tgt, idx, src, axis=0):
    return tgt.at[idx].add(src)

def _segment_sum(src, seg, n):
    return jax.ops.segment_sum(src, seg, n)
kernel_name = 'mk_adaln_attn_ffn_d1_seqx_r8_b3135d'

def setup_inputs(seed: int=0):
    np.random.seed(seed)
    _w = jnp.asarray

    def _rec_inputs():
        import jax
        import jax.numpy as jnp
        _rk = jax.random.key(seed)
        x = -0.000125 + 0.9999 * jax.random.normal(jax.random.fold_in(_rk, 1), (32, 32, 256), jnp.float32)
        _lenS = 32 - jax.random.randint(jax.random.fold_in(_rk, 7), (32,), 0, max(1, 32 // 4) + 1, jnp.int32)
        _lenS2 = 32 - jax.random.randint(jax.random.fold_in(_rk, 8), (32,), 0, max(1, 32 // 4) + 1, jnp.int32)
        itok_B_0_7 = jax.random.randint(jax.random.fold_in(_rk, 11), (32,), 0, 8, jnp.int32)
        fside_8xS_0 = -0.00162727 + 0.0609077 * jax.random.normal(jax.random.fold_in(_rk, 12), (8, 32), jnp.float32)
        itok_B_1_198 = jax.random.randint(jax.random.fold_in(_rk, 13), (32,), 1, 199, jnp.int32)
        return (x, itok_B_0_7, fside_8xS_0, itok_B_1_198)
    x, itok_B_0_7, fside_8xS_0, itok_B_1_198 = _rec_inputs()

    def _L0_cond_setup():
        import jax, jax.numpy as jnp
        import numpy as np
        B, C, T = (64, 32, 256)
        D, N = (32, 8)
        key = jax.random.key(seed)
        k_x, k_s, k_w, k_b = jax.random.split(key, 4)
        scale = 1.0 / np.sqrt(C)
        x = jax.random.normal(k_x, (B, C, T), dtype=jnp.float32)
        subjects = jax.random.randint(k_s, (B,), 0, N, dtype=jnp.int64)
        weights = jax.random.normal(k_w, (N, C, D), dtype=jnp.float32) * scale
        bias = jax.random.normal(k_b, (N, D), dtype=jnp.float32) * scale
        return {'x': x, 'subjects': subjects, 'weights': weights, 'bias': bias}
    _L0_cond_all = _L0_cond_setup()
    _L0_cond_in = {k: v for k, v in _L0_cond_all.items() if k in ('weights',)}
    del _L0_cond_all

    def _L0_attn_setup():
        import jax, jax.numpy as jnp
        import numpy as np
        B, T, C = (2, 256, 256)
        H, KVH = (16, 4)
        HD = C // H
        REP = H // KVH

        def _alibi_slopes(n_head):
            start = 2.0 ** (-2.0 ** (-(np.log2(n_head) - 3.0)))
            return jnp.asarray([start ** (i + 1) for i in range(n_head)], jnp.float32)
        key = jax.random.key(seed)
        ks = jax.random.split(key, 4)
        sc = 0.02
        return {'x': jax.random.normal(ks[0], (B, T, C), jnp.float32), 'Wq': jax.random.normal(ks[1], (C, C), jnp.float32) * sc, 'Wkv': jax.random.normal(ks[2], (C, HD * KVH * 2), jnp.float32) * sc, 'Wo': jax.random.normal(ks[3], (C, C), jnp.float32) * sc, 'bo': jnp.zeros((C,), jnp.float32)}
    _L0_attn_all = _L0_attn_setup()
    _L0_attn_in = {k: v for k, v in _L0_attn_all.items() if k in ('Wq', 'Wkv', 'Wo', 'bo')}
    del _L0_attn_all

    def _L0_cond2_setup():
        import jax, jax.numpy as jnp
        import numpy as np
        B, C, T = (128, 32, 256)
        S, D = (200, 32)
        key = jax.random.key(seed)
        k1, k2, k3 = jax.random.split(key, 3)
        x = jax.random.normal(k1, (B, C, T), dtype=jnp.float32)
        conditions = jax.random.randint(k2, (B,), 0, S, dtype=jnp.int64)
        weights = jax.random.normal(k3, (S, C, D), dtype=jnp.float32) / jnp.sqrt(jnp.float32(C))
        return {'x': x, 'conditions': conditions, 'weights': weights}
    _L0_cond2_all = _L0_cond2_setup()
    _L0_cond2_in = {k: v for k, v in _L0_cond2_all.items() if k in ('weights',)}
    del _L0_cond2_all

    def _L0_ffn_setup():
        import jax, jax.numpy as jnp
        import numpy as np
        DIM_IN = 256
        DIM_HIDDEN = 1024
        key = jax.random.key(seed)
        k_x, k_g, k_u, k_d = jax.random.split(key, 4)
        s_in = 1.0 / np.sqrt(DIM_IN)
        s_hid = 1.0 / np.sqrt(DIM_HIDDEN)
        x = jax.random.normal(k_x, (4, 256, DIM_IN), dtype=jnp.float32)
        w_gate = jax.random.uniform(k_g, (DIM_HIDDEN, DIM_IN), jnp.float32, -s_in, s_in)
        w_up = jax.random.uniform(k_u, (DIM_HIDDEN, DIM_IN), jnp.float32, -s_in, s_in)
        w_down = jax.random.uniform(k_d, (DIM_IN, DIM_HIDDEN), jnp.float32, -s_hid, s_hid)
        return {'x': x, 'w_gate': w_gate, 'w_up': w_up, 'w_down': w_down}
    _L0_ffn_all = _L0_ffn_setup()
    _L0_ffn_in = {k: v for k, v in _L0_ffn_all.items() if k in ('w_gate', 'w_up', 'w_down')}
    del _L0_ffn_all
    return {'x': x, 'itok_B_0_7': itok_B_0_7, 'fside_8xS_0': fside_8xS_0, 'itok_B_1_198': itok_B_1_198, 'L0_cond_weights': _L0_cond_in['weights'], 'L0_attn_Wq': _L0_attn_in['Wq'], 'L0_attn_Wkv': _L0_attn_in['Wkv'], 'L0_attn_Wo': _L0_attn_in['Wo'], 'L0_attn_bo': _L0_attn_in['bo'], 'L0_cond2_weights': _L0_cond2_in['weights'], 'L0_ffn_w_gate': _L0_ffn_in['w_gate'], 'L0_ffn_w_up': _L0_ffn_in['w_up'], 'L0_ffn_w_down': _L0_ffn_in['w_down']}

def reference(x, itok_B_0_7, fside_8xS_0, itok_B_1_198, L0_cond_weights, L0_attn_Wq, L0_attn_Wkv, L0_attn_Wo, L0_attn_bo, L0_cond2_weights, L0_ffn_w_gate, L0_ffn_w_up, L0_ffn_w_down):
    import jax
    import jax.numpy as jnp

    def _L0_cond_ref(x, subjects, weights, bias):
        import jax, jax.numpy as jnp
        import numpy as np
        B, C, T = (64, 32, 256)
        D, N = (32, 8)
        w = weights[subjects]
        b = bias[subjects]
        out = jnp.einsum('bct,bcd->bdt', x, w)
        out = out + b[:, :, None]
        return out

    def _L0_attn_ref(x, Wq, Wkv, Wo, bo):
        import jax, jax.numpy as jnp
        import numpy as np
        B, T, C = (2, 256, 256)
        H, KVH = (16, 4)
        HD = C // H
        REP = H // KVH

        def _alibi_slopes(n_head):
            start = 2.0 ** (-2.0 ** (-(np.log2(n_head) - 3.0)))
            return jnp.asarray([start ** (i + 1) for i in range(n_head)], jnp.float32)
        Bv, Tv, Cv = x.shape
        q = (x @ Wq).reshape(Bv, Tv, H, HD).transpose(0, 2, 1, 3)
        k, v = jnp.split(x @ Wkv, 2, axis=-1)
        k = k.reshape(Bv, Tv, KVH, HD).transpose(0, 2, 1, 3)
        v = v.reshape(Bv, Tv, KVH, HD).transpose(0, 2, 1, 3)
        qg = q.reshape(Bv, REP, KVH, Tv, HD)
        scores = jnp.einsum('brgtd,bgsd->brgts', qg, k) / jnp.sqrt(jnp.float32(HD))
        idx = jnp.arange(Tv)
        diff = (idx[None, :] - idx[:, None]).astype(jnp.float32)
        slopes = _alibi_slopes(H).reshape(REP, KVH)
        bias = jnp.tril(diff)[None, None] * slopes[:, :, None, None]
        causal = idx[None, :] <= idx[:, None]
        scores = jnp.where(causal[None, None, None], scores + bias[None], -jnp.inf)
        attn = jax.nn.softmax(scores, axis=-1)
        out = jnp.einsum('brgts,bgsd->brgtd', attn, v)
        out = out.reshape(Bv, H, Tv, HD).transpose(0, 2, 1, 3).reshape(Bv, Tv, Cv)
        return out @ Wo + bo

    def _L0_cond2_ref(x, conditions, weights):
        import jax, jax.numpy as jnp
        import numpy as np
        B, C, T = (128, 32, 256)
        S, D = (200, 32)
        w = weights[conditions]
        return jnp.einsum('bct,bcd->bdt', x, w)

    def _L0_ffn_ref(x, w_gate, w_up, w_down):
        import jax, jax.numpy as jnp
        import numpy as np
        DIM_IN = 256
        DIM_HIDDEN = 1024
        gate = jnp.einsum('bsd,hd->bsh', x, w_gate)
        up = jnp.einsum('bsd,hd->bsh', x, w_up)
        gated = jax.nn.silu(gate) * up
        return jnp.einsum('bsh,dh->bsd', gated, w_down)
    x = x + _L0_attn_ref(_L0_cond_ref(x, itok_B_0_7, L0_cond_weights, fside_8xS_0), L0_attn_Wq, L0_attn_Wkv, L0_attn_Wo, L0_attn_bo)
    x = x + _L0_ffn_ref(_L0_cond2_ref(x, itok_B_1_198, L0_cond2_weights), L0_ffn_w_gate, L0_ffn_w_up, L0_ffn_w_down)
    return x

_drawn_inputs = setup_inputs


def setup_inputs(seed=0):
    import zlib

    import numpy as np

    out = dict(_drawn_inputs(seed))
    spreads = {'L0_attn_bo': (0.0, 0.1)}
    factors = {'fside_8xS_0': 8.0, 'L0_attn_Wq': 8.0}
    for name, (base, spread) in spreads.items():
        noise = np.random.default_rng([zlib.crc32(name.encode()), seed]).standard_normal(out[name].shape)
        drawn = base * np.exp(spread * noise) if base else spread * noise
        out[name] = jnp.asarray(drawn.astype(out[name].dtype))
    for name, factor in factors.items():
        out[name] = (out[name] * factor).astype(out[name].dtype)
    return out
```

```python
from contextlib import ExitStack

import numpy as np

import concourse.bass as bass
from concourse import mybir

F32 = mybir.dt.float32
F32R = mybir.dt.float32r
I32 = mybir.dt.int32
ALU = mybir.AluOpType
ACT = mybir.ActivationFunctionType
AX_X = mybir.AxisListType.X

P = 128
B, T, C = 32, 32, 256
H, KVH = 16, 4
HD = C // H
REP = H // KVH
NSUBJ, NCOND = 8, 200
HID = 1024
GB = P // T
NG = B // GB
CG = 2
NCH = NG // CG
CB = CG * GB
CT = CG * P
KT = C // P
RH = REP // 2
MT = HID // P
GRING = 4
LAG = 2
MASKED = -1.0e38


def tables():
    p = np.arange(P)
    ident = np.eye(P, dtype=np.float32)
    start = 2.0 ** (-2.0 ** (-(np.log2(H) - 3.0)))
    slopes = np.array([start ** (i + 1) for i in range(H)], np.float32)
    g, t = (p // T)[:, None, None, None], (p % T)[:, None, None, None]
    r2, j, s = np.arange(2)[:, None, None], np.arange(RH)[:, None], np.arange(T)
    slope = slopes[(2 * j + r2) * KVH + g]
    alibi = np.where(s <= t, slope * (s - t).astype(np.float32), np.float32(MASKED))
    alibi = np.broadcast_to(alibi, (P, 2, RH, T)).reshape(P, P).astype(np.float32)
    head = (((p // HD) % KVH)[:, None] == np.arange(KVH)).astype(np.float32)
    batch = ((p // T)[:, None] == np.arange(GB)).astype(np.float32)
    row = (p % T)[:, None].astype(np.float32)
    number = p[:, None].astype(np.float32)
    return np.ascontiguousarray(np.concatenate([ident, alibi, head, batch, row, number], axis=1))


NTAB = 2 * P + KVH + GB + 2


def adaln_attn_ffn(nc, x, index, subject_row, side, table, w_cond, w_cond2, w_qkv, w_o, b_o, w_ffn, out):
    ctx = ExitStack()
    with ctx:
        def sb(name, shape, dt=F32):
            return ctx.enter_context(nc.sbuf_tensor(name, shape, dt))

        def bank(name):
            return ctx.enter_context(nc.psum_tensor(name, [P, 512], F32))

        def sem(name):
            return ctx.enter_context(nc.semaphore(name))

        tab = sb("tab", [P, NTAB])
        ident = tab[:, 0:P]
        alibi = tab[:, P:2 * P]
        head_mask = tab[:, 2 * P:2 * P + KVH]
        batch_mask = tab[:, 2 * P + KVH:2 * P + KVH + GB]
        row_of_p = tab[:, 2 * P + KVH + GB:2 * P + KVH + GB + 1]
        number_of_p = tab[:, 2 * P + KVH + GB + 1:NTAB]
        idx_in = sb("idx_in", [P, 2 * NG], I32)
        idx = sb("idx", [P, 2 * NG], I32)
        subj = sb("subj", [NSUBJ, B], I32)
        side_sb = sb("side_sb", [NSUBJ, T])
        onehot = sb("onehot", [NSUBJ, B])
        side_of = sb("side_of", [NSUBJ, B, T])
        ones = sb("ones", [NSUBJ, P])
        bias_bc = sb("bias_bc", [P, B * T])
        wc1 = sb("wc1", [P, NG, T])
        wc2 = sb("wc2", [P, NG, T])
        w1bd = sb("w1bd", [P, NG, GB, T])
        w2bd = sb("w2bd", [P, NG, GB, T])
        wqkv_sb = sb("wqkv_sb", [P, KT, 2 * C])
        wo_sb = sb("wo_sb", [P, KT, C])
        bo_sb = sb("bo_sb", [P, C])
        wf = sb("wf", [P, MT, 3 * C])
        wf_hi = sb("wf_hi", [P, MT, 3 * C], F32R)
        wf_lo = sb("wf_lo", [P, MT, 3 * C], F32R)
        x_sb = sb("x_sb", [P, NG, C])
        xb = sb("xb", [P, NG, C])
        x1 = sb("x1", [P, NG, C])
        yT = sb("yT", [P, 2, KT, CT])
        qz = sb("qz", [P, 2, CB, 2, RH, T])
        kbd = sb("kbd", [P, 2, CB, KVH, T])
        vbdT = sb("vbdT", [P, 2, CB, KVH, T])
        vbd = sb("vbd", [P, 2, CB, P])
        sc = sb("sc", [P, 2, CB, P])
        mx = sb("mx", [P, 2, CB * REP])
        sm = sb("sm", [P, 2, CB * REP])
        rs = sb("rs", [P, 2, CB * REP])
        pT = sb("pT", [P, 2, CB, P])
        aT = sb("aT", [P, 2, RH, CB, T])
        z_hi = sb("z_hi", [P, 2, KT, CT], F32R)
        z_lo = sb("z_lo", [P, 2, KT, CT], F32R)
        sil = sb("sil", [P, 2, CT])
        gated = sb("gated", [P, GRING, CT])
        g_hi = sb("g_hi", [P, GRING, CT], F32R)
        g_lo = sb("g_lo", [P, GRING, CT], F32R)
        out_sb = sb("out_sb", [P, 2, CG, C])

        bank_yz = bank("bank_yz")
        bank_qo = bank("bank_qo")
        bank_kv = bank("bank_kv")
        bank_sp = [bank("bank_sp0"), bank("bank_sp1")]
        bank_gu = [bank("bank_gu0"), bank("bank_gu1")]
        bank_dn = bank("bank_dn")

        ld_idx, ld_tab, ld_subj, ld_side = sem("ld_idx"), sem("ld_tab"), sem("ld_subj"), sem("ld_side")
        ld_x0, ld_x, ld_wqkv = sem("ld_x0"), sem("ld_x"), sem("ld_wqkv")
        ld_wo, ld_bo = sem("ld_wo"), sem("ld_bo")
        ld_wf = [sem(f"ld_wf{m}") for m in range(MT)]
        got_w1 = [sem(f"got_w1_{c}") for c in range(NCH)]
        got_w2 = [sem(f"got_w2_{c}") for c in range(NCH)]
        stored = [sem(f"stored{n}") for n in range(2)]
        pe_bias, pe_y, pe_q, pe_kv = sem("pe_bias"), sem("pe_y"), sem("pe_q"), sem("pe_kv")
        pe_s, pe_vt, pe_pv = sem("pe_s"), sem("pe_vt"), sem("pe_pv")
        pe_wo, pe_z, pe_gu, pe_dn = sem("pe_wo"), sem("pe_z"), sem("pe_gu"), sem("pe_dn")
        idx_ready, onehot_ready, side_ready = sem("idx_ready"), sem("onehot_ready"), sem("side_ready")
        ones_ready, bias_ready = sem("ones_ready"), sem("bias_ready")
        w1_ready, w2_ready, y_ready = sem("w1_ready"), sem("w2_ready"), sem("y_ready")
        kbd_ready, vbdT_ready = sem("kbd_ready"), sem("vbdT_ready")
        s_turned, s_biased, max_ready = sem("s_turned"), sem("s_biased"), sem("max_ready")
        sum_ready, recip_ready, pT_ready = sem("sum_ready"), sem("recip_ready"), sem("pT_ready")
        x1_ready, zlo_ready, gated_ready = sem("x1_ready"), sem("zlo_ready"), sem("gated_ready")
        out_ready = sem("out_ready")
        q_ready, v_ready, exp_ready, a_ready = sem("q_ready"), sem("v_ready"), sem("exp_ready"), sem("a_ready")
        zhi_ready, silu_ready, ghi_ready, whi_ready = (
            sem("zhi_ready"), sem("silu_ready"), sem("ghi_ready"), sem("whi_ready"))
        qz_zeroed, xb_ready, shifted, normed = sem("qz_zeroed"), sem("xb_ready"), sem("shifted"), sem("normed")
        glo_ready, wlo_ready = sem("glo_ready"), sem("wlo_ready")

        x_rows = x.rearrange("(g p) f -> p g f", p=P)
        out_rows = out.rearrange("(g p) f -> p g f", p=P)

        block = ctx.enter_context(nc.Block())

        @block.sync
        def _(sp):
            sp.dma_start(idx_in[:], index).then_inc(ld_idx, 16)
            sp.dma_start(tab[:], table).then_inc(ld_tab, 16)
            sp.dma_start(subj[:], subject_row).then_inc(ld_subj, 16)
            sp.dma_start(side_sb[:], side).then_inc(ld_side, 16)
            sp.dma_start(x_sb[:, 0:CG, :], x_rows[:, 0:CG, :]).then_inc(ld_x0, 16)
            sp.dma_start(wqkv_sb[:], w_qkv).then_inc(ld_wqkv, 16)
            sp.dma_start(x_sb[:, CG:NG, :], x_rows[:, CG:NG, :]).then_inc(ld_x, 16)
            sp.dma_start(bo_sb[:], b_o).then_inc(ld_bo, 16)
            sp.dma_start(wo_sb[:], w_o).then_inc(ld_wo, 16)
            for m in range(MT):
                sp.dma_start(wf[:, m, :], w_ffn[:, m, :]).then_inc(ld_wf[m], 16)
            for c in range(NCH):
                sp.wait_ge(out_ready, c + 1)
                sp.dma_start(out_rows[:, c * CG:(c + 1) * CG, :], out_sb[:, c % 2]).then_inc(stored[c % 2], 16)
            for n in range(2):
                sp.wait_ge(stored[n], 16 * NCH // 2)

        @block.gpsimd
        def _(pool):
            def gather(table_rows, dst, col, grp, done):
                pool.indirect_dma_start(
                    dst[:, grp, :], None, table_rows,
                    bass.IndirectOffsetOnAxis(ap=idx[:, col + grp:col + grp + 1], axis=0)).then_inc(done, 16)

            def gather1(c):
                for grp in range(c * CG, (c + 1) * CG):
                    gather(w_cond.rearrange("n c d -> (n c) d"), wc1, 0, grp, got_w1[c])

            def gather2(c):
                for grp in range(c * CG, (c + 1) * CG):
                    gather(w_cond2.rearrange("n c d -> (n c) d"), wc2, NG, grp, got_w2[c])

            def add_bo(c):
                pool.wait_ge(ld_x, 16)
                pool.wait_ge(ld_x0, 16)
                pool.wait_ge(ld_bo, 16)
                pool.tensor_tensor(xb[:, c * CG:(c + 1) * CG, :], x_sb[:, c * CG:(c + 1) * CG, :],
                                   bo_sb[:].unsqueeze(1).to_broadcast([P, CG, C]), ALU.add).then_inc(xb_ready, 1)

            def split_weights(m):
                pool.wait_ge(whi_ready, m + 1)
                pool.tensor_tensor(wf_lo[:, m, :], wf[:, m, :], wf_hi[:, m, :].bitcast(F32),
                                   ALU.subtract).then_inc(wlo_ready, 1)

            def shift(c, k):
                n = c * CG + k
                pool.wait_ge(max_ready, n + 1)
                v = sc[:, c % 2, k * GB:(k + 1) * GB, :].rearrange("p b (r s) -> p (b r) s", s=T)
                m = mx[:, c % 2, k * GB * REP:(k + 1) * GB * REP]
                pool.tensor_tensor(v, v, m.unsqueeze(2).to_broadcast([P, GB * REP, T]),
                                   ALU.subtract).then_inc(shifted, 1)

            def norm(c, k):
                n = c * CG + k
                pool.wait_ge(recip_ready, n + 1)
                v = sc[:, c % 2, k * GB:(k + 1) * GB, :].rearrange("p b (r s) -> p (b r) s", s=T)
                m = rs[:, c % 2, k * GB * REP:(k + 1) * GB * REP]
                pool.tensor_tensor(v, v, m.unsqueeze(2).to_broadcast([P, GB * REP, T]),
                                   ALU.mult).then_inc(normed, 1)

            def low_gated(i):
                pool.wait_ge(ghi_ready, i + 1)
                pool.tensor_tensor(g_lo[:, i % GRING, :], gated[:, i % GRING, :],
                                   g_hi[:, i % GRING, :].bitcast(F32), ALU.subtract).then_inc(glo_ready, 1)

            pool.wait_ge(idx_ready, 2)
            gather1(0)
            pool.memset(qz[:].rearrange("p a b r j t -> p (a b r j t)"), 0.0).then_inc(qz_zeroed, 1)
            gather1(1)
            gather2(0)
            shift(0, 0)
            shift(0, 1)
            norm(0, 0)
            norm(0, 1)
            add_bo(0)
            split_weights(0)
            shift(1, 0)
            shift(1, 1)
            split_weights(1)
            norm(1, 0)
            norm(1, 1)
            for c in range(NCH):
                for m in range(MT):
                    low_gated(c * MT + m)
                    if c == 0 and m + 2 < MT:
                        split_weights(m + 2)
                    if m == 0 and c + 1 < NCH:
                        add_bo(c + 1)
                        if c == 0:
                            gather1(2)
                        gather2(c + 1)
                    if m == 7 and c == 0:
                        gather1(3)
                    if c + 2 < NCH and m in (3, 4):
                        shift(c + 2, m - 3)
                    if c + 2 < NCH and m in (6, 7):
                        norm(c + 2, m - 6)

        @block.scalar
        def _(act):
            def round_weights(m):
                act.wait_ge(ld_wf[m], 16)
                act.copy(wf_hi[:, m, :], wf[:, m, :]).then_inc(whi_ready, 1)

            def q_out(c):
                act.wait_ge(pe_q, c + 1)
                if c == 0:
                    act.wait_ge(qz_zeroed, 1)
                q = bank_qo[:].rearrange("p (j b t) -> p b j t", j=RH, b=CB)
                for r2 in range(2):
                    rows = slice(64 * r2, 64 * r2 + 64)
                    last = act.activation(qz[rows, c % 2, :, r2, :, :], q[rows], ACT.Copy, scale=HD ** -0.5)
                last.then_inc(q_ready, 1)

            def v_out(c, k):
                act.wait_ge(pe_vt, c * CG + k + 1)
                act.copy(vbd[:, c % 2, k * GB:(k + 1) * GB, :],
                         bank_kv[:].rearrange("p (b n) -> p b n", b=GB)).then_inc(v_ready, 1)

            def exp(c, k):
                act.wait_ge(shifted, c * CG + k + 1)
                v = sc[:, c % 2, k * GB:(k + 1) * GB, :]
                act.activation(v, v, ACT.Exp).then_inc(exp_ready, 1)

            def a_out(c, k):
                act.wait_ge(pe_pv, c * CG + k + 1)
                o = bank_sp[k][:].rearrange("p (b r j t) -> p r j b t", b=GB, r=2, j=RH)
                for r2 in range(2):
                    rows = slice(64 * r2, 64 * r2 + 64)
                    last = act.copy(aT[rows, c % 2, :, k * GB:(k + 1) * GB, :], o[rows, r2])
                last.then_inc(a_ready, 1)

            def z_out(c):
                act.wait_ge(pe_z, c + 1)
                act.copy(z_hi[:, c % 2], bank_yz[:].rearrange("p (f t) -> p f t", f=KT)).then_inc(zhi_ready, 1)

            def silu(i):
                act.wait_ge(pe_gu, i + 1)
                act.activation(sil[:, i % 2, :], bank_gu[i % 2][:, 0:CT], ACT.Silu).then_inc(silu_ready, 1)

            def round_gated(i):
                act.wait_ge(gated_ready, i + 1)
                act.copy(g_hi[:, i % GRING, :], gated[:, i % GRING, :]).then_inc(ghi_ready, 1)

            q_out(0)
            v_out(0, 0)
            v_out(0, 1)
            round_weights(0)
            q_out(1)
            exp(0, 0)
            exp(0, 1)
            v_out(1, 0)
            v_out(1, 1)
            round_weights(1)
            exp(1, 0)
            exp(1, 1)
            a_out(0, 0)
            a_out(0, 1)
            z_out(0)
            for c in range(NCH):
                for m in range(MT):
                    i = c * MT + m
                    silu(i)
                    if c == 0 and m + 2 < MT:
                        round_weights(m + 2)
                    if c + 2 < NCH and m == 1:
                        q_out(c + 2)
                    if c + 2 < NCH and m in (2, 3):
                        v_out(c + 2, m - 2)
                    if c + 2 < NCH and m == 5:
                        exp(c + 2, 0)
                        exp(c + 2, 1)
                    if c + 1 < NCH and m == 4:
                        a_out(c + 1, 0)
                        a_out(c + 1, 1)
                    if c + 1 < NCH and m == 6:
                        z_out(c + 1)
                    round_gated(i)

        @block.vector
        def _(dve):
            def block_diagonal(c, src, dst, got, done):
                dve.wait_ge(got[c], 16 * CG)
                g = slice(c * CG, (c + 1) * CG)
                dve.tensor_tensor(dst[:, g], src[:, g].unsqueeze(2).to_broadcast([P, CG, GB, T]),
                                  batch_mask.unsqueeze(1).unsqueeze(3).to_broadcast([P, CG, GB, T]),
                                  ALU.mult).then_inc(done, 1)

            def bias_out(h):
                dve.wait_ge(pe_bias, h + 1)
                dve.tensor_copy(bias_bc[:, 512 * h:512 * h + 512], bank_sp[h][:]).then_inc(bias_ready, 1)

            def y_out(c):
                dve.wait_ge(pe_y, c + 1)
                dve.wait_ge(bias_ready, 2)
                dve.tensor_tensor(yT[:, c % 2], bank_yz[:].rearrange("p (f t) -> p f t", f=KT),
                                  bias_bc[:, c * CT:(c + 1) * CT].unsqueeze(1).to_broadcast([P, KT, CT]),
                                  ALU.add).then_inc(y_ready, 1)

            def kv_out(c):
                dve.wait_ge(pe_kv, c + 1)
                for n, (dst, done) in enumerate(((kbd, kbd_ready), (vbdT, vbdT_ready))):
                    src = bank_kv[:, n * CT:(n + 1) * CT].rearrange("p (b t) -> p b t", b=CB)
                    dve.tensor_tensor(dst[:, c % 2], src.unsqueeze(2).to_broadcast([P, CB, KVH, T]),
                                      head_mask.unsqueeze(1).unsqueeze(3).to_broadcast([P, CB, KVH, T]),
                                      ALU.mult).then_inc(done, 1)

            def row_max(c, k):
                n = c * CG + k
                v = sc[:, c % 2, k * GB:(k + 1) * GB, :]
                dve.wait_ge(pe_s, n + 1)
                dve.transpose(v.rearrange("p b n -> p (b n)"), bank_sp[k][:]).then_inc(s_turned, 1)
                dve.wait_ge(s_turned, n + 1)
                dve.tensor_tensor(v, v, alibi.unsqueeze(1).to_broadcast([P, GB, P]), ALU.add).then_inc(s_biased, 1)
                dve.wait_ge(s_biased, n + 1)
                dve.tensor_reduce(mx[:, c % 2, k * GB * REP:(k + 1) * GB * REP],
                                  v.rearrange("p b (r s) -> p (b r) s", s=T), AX_X, ALU.max).then_inc(max_ready, 1)

            def row_sum(c, k):
                n = c * CG + k
                cols = slice(k * GB * REP, (k + 1) * GB * REP)
                dve.wait_ge(exp_ready, n + 1)
                dve.tensor_reduce(sm[:, c % 2, cols],
                                  sc[:, c % 2, k * GB:(k + 1) * GB, :].rearrange("p b (r s) -> p (b r) s", s=T),
                                  AX_X, ALU.add).then_inc(sum_ready, 1)
                dve.wait_ge(sum_ready, n + 1)
                dve.reciprocal(rs[:, c % 2, cols], sm[:, c % 2, cols]).then_inc(recip_ready, 1)

            def turn_probs(c, k):
                dve.wait_ge(normed, c * CG + k + 1)
                b = slice(k * GB, (k + 1) * GB)
                dve.transpose(pT[:, c % 2, b, :].rearrange("p b n -> p (b n)"),
                              sc[:, c % 2, b, :].rearrange("p b n -> p (b n)")).then_inc(pT_ready, 1)

            def x1_out(c):
                g = slice(c * CG, (c + 1) * CG)
                dve.wait_ge(pe_wo, c + 1)
                dve.wait_ge(xb_ready, c + 1)
                dve.tensor_tensor(x1[:, g], bank_qo[:].rearrange("p (g f) -> p g f", g=CG), xb[:, g],
                                  ALU.add).then_inc(x1_ready, 1)

            def z_low(c):
                dve.wait_ge(zhi_ready, c + 1)
                dve.tensor_tensor(z_lo[:, c % 2], bank_yz[:].rearrange("p (f t) -> p f t", f=KT),
                                  z_hi[:, c % 2].bitcast(F32), ALU.subtract).then_inc(zlo_ready, 1)

            def gate(i):
                dve.wait_ge(silu_ready, i + 1)
                if i >= GRING:
                    dve.wait_ge(glo_ready, i - GRING + 1)
                dve.tensor_tensor(gated[:, i % GRING, :], bank_gu[i % 2][:, CT:2 * CT], sil[:, i % 2, :],
                                  ALU.mult).then_inc(gated_ready, 1)

            def result(c):
                g = slice(c * CG, (c + 1) * CG)
                dve.wait_ge(pe_dn, c + 1)
                if c >= 2:
                    dve.wait_ge(stored[c % 2], 16 * (c // 2))
                dve.tensor_tensor(out_sb[:, c % 2], bank_dn[:].rearrange("p (g f) -> p g f", g=CG), x1[:, g],
                                  ALU.add).then_inc(out_ready, 1)

            dve.memset(ones[:], 1.0).then_inc(ones_ready, 1)
            dve.wait_ge(ld_idx, 16)
            dve.wait_ge(ld_tab, 16)
            for n in range(2):
                cols = slice(n * NG, (n + 1) * NG)
                dve.tensor_scalar(idx[:, cols], idx_in[:, cols], float(T), row_of_p, ALU.mult,
                                  ALU.add).then_inc(idx_ready, 1)
            dve.wait_ge(ld_subj, 16)
            dve.tensor_scalar(onehot[:], subj[:], number_of_p[0:NSUBJ], None, ALU.is_equal).then_inc(onehot_ready, 1)
            dve.wait_ge(onehot_ready, 1)
            dve.wait_ge(ld_side, 16)
            dve.tensor_tensor(side_of[:], onehot[:].unsqueeze(2).to_broadcast([NSUBJ, B, T]),
                              side_sb[:].unsqueeze(1).to_broadcast([NSUBJ, B, T]), ALU.mult).then_inc(side_ready, 1)
            block_diagonal(0, wc1, w1bd, got_w1, w1_ready)
            bias_out(0)
            bias_out(1)
            y_out(0)
            kv_out(0)
            row_max(0, 0)
            row_max(0, 1)
            block_diagonal(1, wc1, w1bd, got_w1, w1_ready)
            y_out(1)
            kv_out(1)
            row_sum(0, 0)
            row_sum(0, 1)
            row_max(1, 0)
            row_max(1, 1)
            turn_probs(0, 0)
            turn_probs(0, 1)
            block_diagonal(0, wc2, w2bd, got_w2, w2_ready)
            row_sum(1, 0)
            row_sum(1, 1)
            x1_out(0)
            z_low(0)
            turn_probs(1, 0)
            turn_probs(1, 1)
            for c in range(NCH):
                for m in range(MT):
                    gate(c * MT + m)
                    if m == 0 and c == 0:
                        block_diagonal(2, wc1, w1bd, got_w1, w1_ready)
                    if m == 7 and c == 0:
                        block_diagonal(3, wc1, w1bd, got_w1, w1_ready)
                    if m == 1 and c > 0:
                        result(c - 1)
                    if c + 2 < NCH and m == 0:
                        y_out(c + 2)
                    if c + 2 < NCH and m == 1:
                        kv_out(c + 2)
                    if c + 2 < NCH and m in (2, 3):
                        row_max(c + 2, m - 2)
                    if c + 1 < NCH and m == 4:
                        block_diagonal(c + 1, wc2, w2bd, got_w2, w2_ready)
                    if c + 1 < NCH and m == 5:
                        x1_out(c + 1)
                    if c + 2 < NCH and m in (5, 6):
                        row_sum(c + 2, m - 5)
                    if c + 1 < NCH and m == 6:
                        z_low(c + 1)
                    if c + 2 < NCH and m == 7:
                        turn_probs(c + 2, 0)
                        turn_probs(c + 2, 1)
            result(NCH - 1)

        @block.tensor
        def _(pe):
            def bias_mm():
                pe.wait_ge(side_ready, 1)
                pe.wait_ge(ones_ready, 1)
                for h in range(2):
                    pe.matmul(bank_sp[h][:], ones[:], side_of[:, h * 16:(h + 1) * 16, :].rearrange("n b d -> n (b d)"),
                              start=True, stop=True).then_inc(pe_bias, 1)

            def y_mm(c):
                pe.wait_ge(ld_x0 if c == 0 else ld_x, 16)
                pe.wait_ge(w1_ready, c + 1)
                if c > 1:
                    pe.wait_ge(zlo_ready, c - 1)
                for k in range(CG):
                    for ft in range(KT):
                        last = pe.matmul(bank_yz[:, ft * CT + k * P:ft * CT + (k + 1) * P],
                                         x_sb[:, c * CG + k, ft * P:(ft + 1) * P],
                                         w1bd[:, c * CG + k].rearrange("p b d -> p (b d)"), start=True, stop=True)
                last.then_inc(pe_y, 1)

            def q_mm(c):
                pe.wait_ge(y_ready, c + 1)
                pe.wait_ge(ld_wqkv, 16)
                if c > 1:
                    pe.wait_ge(x1_ready, c - 1)
                for j in range(RH):
                    for ft in range(KT):
                        last = pe.matmul(bank_qo[:, j * CT:(j + 1) * CT], wqkv_sb[:, ft, j * P:(j + 1) * P],
                                         yT[:, c % 2, ft, :], start=(ft == 0), stop=(ft == KT - 1))
                last.then_inc(pe_q, 1)

            def kv_mm(c):
                if c > 0:
                    pe.wait_ge(v_ready, c * CG)
                for n in range(2):
                    for ft in range(KT):
                        last = pe.matmul(bank_kv[:, n * CT:(n + 1) * CT],
                                         wqkv_sb[:, ft, C + n * P:C + (n + 1) * P],
                                         yT[:, c % 2, ft, :], start=(ft == 0), stop=(ft == KT - 1))
                last.then_inc(pe_kv, 1)

            def score_mm(c, k, bank_free, count):
                pe.wait_ge(q_ready, c + 1)
                pe.wait_ge(kbd_ready, c + 1)
                pe.wait_ge(bank_free, count)
                for b in range(GB):
                    last = pe.matmul(bank_sp[k][:, b * P:(b + 1) * P],
                                     kbd[:, c % 2, k * GB + b].rearrange("p g s -> p (g s)"),
                                     qz[:, c % 2, k * GB + b].rearrange("p r j t -> p (r j t)"),
                                     start=True, stop=True)
                last.then_inc(pe_s, 1)

            def turn_v(c, k):
                pe.wait_ge(vbdT_ready, c + 1)
                if k > 0:
                    pe.wait_ge(v_ready, c * CG + k)
                for b in range(GB):
                    last = pe.transpose(bank_kv[:, b * P:(b + 1) * P],
                                        vbdT[:, c % 2, k * GB + b].rearrange("p g s -> p (g s)"), ident)
                last.then_inc(pe_vt, 1)

            def pv_mm(c, k, scores_read):
                pe.wait_ge(pT_ready, c * CG + k + 1)
                pe.wait_ge(v_ready, c * CG + k + 1)
                pe.wait_ge(s_turned, scores_read)
                for b in range(GB):
                    last = pe.matmul(bank_sp[k][:, b * P:(b + 1) * P], vbd[:, c % 2, k * GB + b, :],
                                     pT[:, c % 2, k * GB + b, :], start=True, stop=True)
                last.then_inc(pe_pv, 1)

            def wo_mm(c):
                pe.wait_ge(a_ready, (c + 1) * CG)
                pe.wait_ge(ld_wo, 16)
                pe.wait_ge(q_ready, min(c + 2, NCH))
                for k in range(CG):
                    for j in range(RH):
                        last = pe.matmul(bank_qo[:, k * C:(k + 1) * C],
                                         aT[:, c % 2, j, k * GB:(k + 1) * GB, :].rearrange("p b t -> p (b t)"),
                                         wo_sb[:, j, :], start=(j == 0), stop=(j == RH - 1))
                last.then_inc(pe_wo, 1)

            def z_mm(c):
                pe.wait_ge(x1_ready, c + 1)
                pe.wait_ge(w2_ready, c + 1)
                for k in range(CG):
                    for ft in range(KT):
                        last = pe.matmul(bank_yz[:, ft * CT + k * P:ft * CT + (k + 1) * P],
                                         x1[:, c * CG + k, ft * P:(ft + 1) * P],
                                         w2bd[:, c * CG + k].rearrange("p b d -> p (b d)"), start=True, stop=True)
                last.then_inc(pe_z, 1)

            def up_mm(i):
                c, m = i // MT, i % MT
                pe.wait_ge(zlo_ready, c + 1)
                pe.wait_ge(wlo_ready, m + 1)
                if i > 1:
                    pe.wait_ge(gated_ready, i - 1)
                for n in range(2):
                    at = 0
                    for ft in range(KT):
                        cols = slice((n * KT + ft) * P, (n * KT + ft + 1) * P)
                        for w, z in ((wf_hi, z_hi), (wf_hi, z_lo), (wf_lo, z_hi)):
                            last = pe.matmul(bank_gu[i % 2][:, n * CT:(n + 1) * CT], w[:, m, cols],
                                             z[:, c % 2, ft, :], start=(at == 0), stop=(at == 3 * KT - 1))
                            at += 1
                last.then_inc(pe_gu, 1)

            def down_mm(i):
                c, m = i // MT, i % MT
                pe.wait_ge(glo_ready, i + 1)
                if m == 0 and c > 0:
                    pe.wait_ge(out_ready, c)
                for k in range(CG):
                    for n, (g, w) in enumerate(((g_hi, wf_hi), (g_hi, wf_lo), (g_lo, wf_hi))):
                        last = pe.matmul(bank_dn[:, k * C:(k + 1) * C], g[:, i % GRING, k * P:(k + 1) * P],
                                         w[:, m, 2 * C:3 * C], start=(m == 0 and k == 0 and n == 0),
                                         stop=(m == MT - 1 and n == 2), skip_group_check=True)
                if m == MT - 1:
                    last.then_inc(pe_dn, 1)

            pe.wait_ge(ld_tab, 16)
            bias_mm()
            y_mm(0)
            q_mm(0)
            kv_mm(0)
            score_mm(0, 0, bias_ready, 1)
            score_mm(0, 1, bias_ready, 2)
            turn_v(0, 0)
            turn_v(0, 1)
            y_mm(1)
            q_mm(1)
            kv_mm(1)
            score_mm(1, 0, s_turned, 1)
            score_mm(1, 1, s_turned, 2)
            turn_v(1, 0)
            turn_v(1, 1)
            pv_mm(0, 0, 3)
            pv_mm(0, 1, 4)
            wo_mm(0)
            z_mm(0)
            for i in range(NCH * MT + LAG):
                c, m = i // MT, i % MT
                if i < NCH * MT:
                    up_mm(i)
                if i >= LAG:
                    down_mm(i - LAG)
                if c + 2 < NCH:
                    if m == 0:
                        y_mm(c + 2)
                    if m == 1:
                        q_mm(c + 2)
                        kv_mm(c + 2)
                    if m in (2, 3):
                        score_mm(c + 2, m - 2, a_ready, (c + 1) * CG - 1 + (m - 2))
                        turn_v(c + 2, m - 2)
                if c + 1 < NCH:
                    if m == 4:
                        scores_read = (min(c + 2, NCH - 1) + 1) * CG
                        pv_mm(c + 1, 0, scores_read - 1)
                        pv_mm(c + 1, 1, scores_read)
                    if m == 5:
                        wo_mm(c + 1)
                    if m == 6:
                        z_mm(c + 1)


def kernel(**inputs):
    import concourse.bacc as bacc
    from concourse.bass_utils import run_bass_kernel_spmd

    def lay(a):
        return np.ascontiguousarray(a)

    a = {k: np.asarray(v) for k, v in inputs.items()}
    x = a["x"].reshape(B * T, C)
    index = [np.repeat(a[n].reshape(NG, GB).T, T, axis=0) for n in ("itok_B_0_7", "itok_B_1_198")]
    wk, wv = a["L0_attn_Wkv"][:, :KVH * HD], a["L0_attn_Wkv"][:, KVH * HD:]
    w_qkv = np.concatenate([a["L0_attn_Wq"], wk, wk, wv, wv], axis=1).reshape(KT, P, 2 * C)
    gate_up = [a[n].reshape(MT, P, KT, P).transpose(3, 0, 2, 1).reshape(P, MT, C)
               for n in ("L0_ffn_w_gate", "L0_ffn_w_up")]
    down = a["L0_ffn_w_down"].reshape(C, MT, P).transpose(2, 1, 0)
    arrays = {
        "x": lay(x),
        "index": lay(np.concatenate(index, axis=1)),
        "subject_row": lay(np.broadcast_to(a["itok_B_0_7"], (NSUBJ, B))),
        "side": lay(a["fside_8xS_0"]),
        "table": tables(),
        "w_cond": lay(a["L0_cond_weights"]),
        "w_cond2": lay(a["L0_cond2_weights"]),
        "w_qkv": lay(w_qkv.transpose(1, 0, 2)),
        "w_o": lay(a["L0_attn_Wo"].reshape(KT, P, C).transpose(1, 0, 2)),
        "b_o": lay(np.broadcast_to(a["L0_attn_bo"], (P, C))),
        "w_ffn": lay(np.concatenate(gate_up + [down], axis=2)),
    }
    nc = bacc.Bacc("TRN2", target_bir_lowering=False, num_devices=1)
    aps = [nc.dram_tensor(f"in_{k}", v.shape, mybir.dt.from_np(v.dtype), kind="ExternalInput").ap()
           for k, v in arrays.items()]
    out = nc.dram_tensor("out_x", (B * T, C), F32, kind="ExternalOutput").ap()
    adaln_attn_ffn(nc, *aps, out)
    r = run_bass_kernel_spmd(nc, [{f"in_{k}": v for k, v in arrays.items()}], core_ids=[0])
    return r.results[0]["out_x"].reshape(B, T, C)
```

```python
from contextlib import ExitStack

import numpy as np

import concourse.bass as bass
from concourse import mybir

F32 = mybir.dt.float32
F32R = mybir.dt.float32r
I32 = mybir.dt.int32
BF16 = mybir.dt.bfloat16
ALU = mybir.AluOpType
ACT = mybir.ActivationFunctionType
AX_X = mybir.AxisListType.X

P = 128
B, T, C = 32, 32, 256
H, KVH = 16, 4
HD = C // H
REP = H // KVH
NSUBJ, NCOND = 8, 200
HID = 1024
GB = P // T
NG = B // GB
CG = 2
NCH = NG // CG
CB = CG * GB
CT = CG * P
KT = C // P
RH = REP // 2
MT = HID // P
GRING = 6
DVE_LOW = 3
WARM = (12, 0, 0, 0, 0, 0)
LAG = 4
MASKED = -1.0e38


def tables():
    p = np.arange(P)
    ident = np.eye(P, dtype=np.float32)
    start = 2.0 ** (-2.0 ** (-(np.log2(H) - 3.0)))
    slopes = np.array([start ** (i + 1) for i in range(H)], np.float32)
    g, t = (p // T)[:, None, None, None], (p % T)[:, None, None, None]
    r2, j, s = np.arange(2)[:, None, None], np.arange(RH)[:, None], np.arange(T)
    slope = slopes[(2 * j + r2) * KVH + g]
    alibi = np.where(s <= t, slope * (s - t).astype(np.float32), np.float32(MASKED))
    alibi = np.broadcast_to(alibi, (P, 2, RH, T)).reshape(P, P).astype(np.float32)
    head = (((p // HD) % KVH)[:, None] == np.arange(KVH)).astype(np.float32)
    batch = ((p // T)[:, None] == np.arange(GB)).astype(np.float32)
    number = p[:, None].astype(np.float32)
    return np.ascontiguousarray(np.concatenate([ident, alibi, head, batch, number], axis=1))


NTAB = 2 * P + KVH + GB + 1


def adaln_attn_ffn(nc, x, index, subject_row, side, table, w_cond, w_cond2, w_qkv, w_o, b_o, w_ffn, out):
    ctx = ExitStack()
    with ctx:
        def sb(name, shape, dt=F32):
            return ctx.enter_context(nc.sbuf_tensor(name, shape, dt))

        def bank(name):
            return ctx.enter_context(nc.psum_tensor(name, [P, 512], F32))

        def sem(name):
            return ctx.enter_context(nc.semaphore(name))

        tab = sb("tab", [P, NTAB])
        ident = tab[:, 0:P]
        alibi = tab[:, P:2 * P]
        head_mask = tab[:, 2 * P:2 * P + KVH]
        batch_mask = tab[:, 2 * P + KVH:2 * P + KVH + GB]
        number_of_p = tab[:, 2 * P + KVH + GB:NTAB]
        idx_in = sb("idx_in", [P, 2 * NG + 1], I32)
        idx = sb("idx", [P, 2 * NG], I32)
        subj = sb("subj", [NSUBJ, B], I32)
        side_sb = sb("side_sb", [NSUBJ, T])
        onehot = sb("onehot", [NSUBJ, B])
        side_of = sb("side_of", [NSUBJ, B, T])
        ones = sb("ones", [NSUBJ, P])
        bias_bc = sb("bias_bc", [P, B * T])
        wc1 = sb("wc1", [P, NG, T])
        wc2 = sb("wc2", [P, NG, T])
        w1bd = sb("w1bd", [P, NG, GB, T])
        w2bd = sb("w2bd", [P, NG, GB, T])
        wqkv_sb = sb("wqkv_sb", [P, KT, 2 * C])
        wo_sb = sb("wo_sb", [P, KT, C])
        bo_sb = sb("bo_sb", [P, C])
        wf = sb("wf", [P, MT, 3 * C])
        wf_hi = sb("wf_hi", [P, MT, 3 * C], F32R)
        wf_lo = sb("wf_lo", [P, MT, 3 * C], F32R)
        x_sb = sb("x_sb", [P, NG, C])
        x1 = sb("x1", [P, NG, C])
        yT = sb("yT", [P, 2, KT, CT])
        qz = sb("qz", [P, 2, CB, 2, RH, T])
        kbd = sb("kbd", [P, 2, CB, KVH, T])
        vbdT = sb("vbdT", [P, 2, CB, KVH, T])
        vbd = sb("vbd", [P, 2, CB, P])
        sc = sb("sc", [P, 2, CB, P])
        mx = sb("mx", [P, 2, CB * REP])
        sm = sb("sm", [P, 2, CB * REP])
        rs = sb("rs", [P, 2, CB * REP])
        pT = sb("pT", [P, 2, CB, P])
        aT = sb("aT", [P, 2, RH, CB, T])
        z_hi = sb("z_hi", [P, 2, KT, CT], F32R)
        z_lo = sb("z_lo", [P, 2, KT, CT], F32R)
        th = sb("th", [P, 2, CT])
        silu2 = sb("silu2", [P, 2, CT])
        gated = sb("gated", [P, GRING, CT])
        g_hi = sb("g_hi", [P, GRING, CT], F32R)
        g_lo = sb("g_lo", [P, GRING, CT], F32R)
        out_sb = sb("out_sb", [P, 2, CG, C])

        warm = sb("warm", [P, 512], BF16)

        bank_yz = bank("bank_yz")
        bank_qo = bank("bank_qo")
        bank_kv = bank("bank_kv")
        bank_sp = [bank("bank_sp0"), bank("bank_sp1")]
        bank_gu = [bank("bank_gu0"), bank("bank_gu1")]
        bank_dn = bank("bank_dn")

        ld_idx, ld_tab, ld_subj, ld_side = sem("ld_idx"), sem("ld_tab"), sem("ld_subj"), sem("ld_side")
        ld_x = [sem("ld_x0"), sem("ld_x1"), sem("ld_x23")]
        ld_wqkv = sem("ld_wqkv")
        ld_wo, ld_bo = sem("ld_wo"), sem("ld_bo")
        ld_wf = [sem(f"ld_wf{m}") for m in range(MT)]
        got_w1 = [sem(f"got_w1_{c}") for c in range(NCH)]
        got_w2 = [sem(f"got_w2_{c}") for c in range(NCH)]
        stored = [sem(f"stored{n}") for n in range(2)]
        pe_bias, pe_y, pe_q, pe_kv = sem("pe_bias"), sem("pe_y"), sem("pe_q"), sem("pe_kv")
        pe_s, pe_vt, pe_pv = sem("pe_s"), sem("pe_vt"), sem("pe_pv")
        pe_wo, pe_z, pe_gu, pe_dn = sem("pe_wo"), sem("pe_z"), sem("pe_gu"), sem("pe_dn")
        warm_ready, idx_ready, onehot_ready, side_ready = (
            sem("warm_ready"), sem("idx_ready"), sem("onehot_ready"), sem("side_ready"))
        ones_ready, bias_ready = sem("ones_ready"), sem("bias_ready")
        w1_ready, w2_ready, y_ready = sem("w1_ready"), sem("w2_ready"), sem("y_ready")
        kbd_ready, vbdT_ready = sem("kbd_ready"), sem("vbdT_ready")
        s_turned, s_biased, max_ready = sem("s_turned"), sem("s_biased"), sem("max_ready")
        sum_ready, recip_ready, pT_ready = sem("sum_ready"), sem("recip_ready"), sem("pT_ready")
        x1_ready, zlo_ready, silu_ready, gated_ready = (
            sem("x1_ready"), sem("zlo_ready"), sem("silu_ready"), sem("gated_ready"))
        out_ready, wlo_dve = sem("out_ready"), sem("wlo_dve")
        q_ready, v_ready, exp_ready, a_ready = sem("q_ready"), sem("v_ready"), sem("exp_ready"), sem("a_ready")
        zhi_ready, tanh_ready, ghi_ready, whi_ready = (
            sem("zhi_ready"), sem("tanh_ready"), sem("ghi_ready"), sem("whi_ready"))
        qz_zeroed, xb_ready, shifted, normed = sem("qz_zeroed"), sem("xb_ready"), sem("shifted"), sem("normed")
        glo_ready, wlo_pool = sem("glo_ready"), sem("wlo_pool")

        BIAS_PARTS = [(slice(0, CT), bank_sp[0]), (slice(CT, 2 * CT), bank_gu[0]), (slice(2 * CT, 4 * CT), bank_gu[1])]

        x_rows = x.rearrange("(g p) f -> p g f", p=P)
        out_rows = out.rearrange("(g p) f -> p g f", p=P)

        block = ctx.enter_context(nc.Block())

        @block.sync
        def _(sp):
            sp.dma_start(idx_in[:], index).then_inc(ld_idx, 16)
            sp.dma_start(x_sb[:, 0:CG, :], x_rows[:, 0:CG, :]).then_inc(ld_x[0], 16)
            sp.dma_start(tab[:], table).then_inc(ld_tab, 16)
            sp.dma_start(subj[:], subject_row).then_inc(ld_subj, 16)
            sp.dma_start(side_sb[:], side).then_inc(ld_side, 16)
            sp.dma_start(wqkv_sb[:], w_qkv).then_inc(ld_wqkv, 16)
            sp.wait_ge(got_w1[0], 16 * CG)
            sp.dma_start(x_sb[:, CG:2 * CG, :], x_rows[:, CG:2 * CG, :]).then_inc(ld_x[1], 16)
            for m in range(MT):
                sp.dma_start(wf[:, m, :], w_ffn[:, m, :]).then_inc(ld_wf[m], 16)
                if m == 3:
                    sp.dma_start(bo_sb[:], b_o).then_inc(ld_bo, 16)
                    sp.dma_start(wo_sb[:], w_o).then_inc(ld_wo, 16)
            sp.dma_start(x_sb[:, 2 * CG:NG, :], x_rows[:, 2 * CG:NG, :]).then_inc(ld_x[2], 16)
            for c in range(NCH):
                sp.wait_ge(out_ready, c + 1)
                sp.dma_start(out_rows[:, c * CG:(c + 1) * CG, :], out_sb[:, c % 2]).then_inc(stored[c % 2], 16)
            for n in range(2):
                sp.wait_ge(stored[n], 16 * NCH // 2)

        @block.gpsimd
        def _(pool):
            def gather(table_rows, dst, col, grp, done):
                pool.indirect_dma_start(
                    dst[:, grp, :], None, table_rows,
                    bass.IndirectOffsetOnAxis(ap=idx[:, col + grp:col + grp + 1], axis=0)).then_inc(done, 16)

            def gather1(c):
                for grp in range(c * CG, (c + 1) * CG):
                    gather(w_cond.rearrange("n c d -> (n c) d"), wc1, 0, grp, got_w1[c])

            def gather2(c):
                for grp in range(c * CG, (c + 1) * CG):
                    gather(w_cond2.rearrange("n c d -> (n c) d"), wc2, NG, grp, got_w2[c])

            def add_bo(c):
                pool.wait_ge(ld_x[min(c, 2)], 16)
                pool.wait_ge(ld_bo, 16)
                pool.tensor_tensor(x1[:, c * CG:(c + 1) * CG, :], x_sb[:, c * CG:(c + 1) * CG, :],
                                   bo_sb[:].unsqueeze(1).to_broadcast([P, CG, C]), ALU.add).then_inc(xb_ready, 1)

            def shift(c, k):
                n = c * CG + k
                pool.wait_ge(max_ready, n + 1)
                v = sc[:, c % 2, k * GB:(k + 1) * GB, :].rearrange("p b (r s) -> p (b r) s", s=T)
                m = mx[:, c % 2, k * GB * REP:(k + 1) * GB * REP]
                pool.tensor_tensor(v, v, m.unsqueeze(2).to_broadcast([P, GB * REP, T]),
                                   ALU.subtract).then_inc(shifted, 1)

            def norm(c, k):
                n = c * CG + k
                pool.wait_ge(recip_ready, n + 1)
                v = sc[:, c % 2, k * GB:(k + 1) * GB, :].rearrange("p b (r s) -> p (b r) s", s=T)
                m = rs[:, c % 2, k * GB * REP:(k + 1) * GB * REP]
                pool.tensor_tensor(v, v, m.unsqueeze(2).to_broadcast([P, GB * REP, T]),
                                   ALU.mult).then_inc(normed, 1)

            def low_weights(m):
                pool.wait_ge(whi_ready, m + 1)
                pool.tensor_tensor(wf_lo[:, m, :], wf[:, m, :], wf_hi[:, m, :].bitcast(F32),
                                   ALU.subtract).then_inc(wlo_pool, 1)

            def low_gated(i):
                pool.wait_ge(ghi_ready, i + 1)
                pool.tensor_tensor(g_lo[:, i % GRING, :], gated[:, i % GRING, :],
                                   g_hi[:, i % GRING, :].bitcast(F32), ALU.subtract).then_inc(glo_ready, 1)

            pool.memset(qz[:].rearrange("p a b r j t -> p (a b r j t)"), 0.0).then_inc(qz_zeroed, 1)
            pool.wait_ge(idx_ready, 1)
            gather1(0)
            gather1(1)
            gather2(0)
            gather1(2)
            gather2(1)
            gather1(3)
            gather2(2)
            gather2(3)
            shift(0, 0)
            shift(0, 1)
            norm(0, 0)
            norm(0, 1)
            add_bo(0)
            for m in range(DVE_LOW, DVE_LOW + 2):
                low_weights(m)
            shift(1, 0)
            for m in range(DVE_LOW + 2, MT):
                low_weights(m)
            shift(1, 1)
            for c in range(NCH):
                for m in range(MT):
                    if c + 1 < NCH:
                        if m in (1, 2) and c > 0:
                            shift(c + 1, m - 1)
                        if m in (3, 4):
                            norm(c + 1, m - 3)
                        if m == 5:
                            add_bo(c + 1)
                    if c * MT + m > 0:
                        low_gated(c * MT + m - 1)
            low_gated(NCH * MT - 1)

        @block.scalar
        def _(act):
            def round_weights(m):
                act.wait_ge(ld_wf[m], 16)
                act.copy(wf_hi[:, m, :], wf[:, m, :]).then_inc(whi_ready, 1)

            def q_out(c):
                act.wait_ge(pe_q, c + 1)
                if c == 0:
                    act.wait_ge(qz_zeroed, 1)
                q = bank_qo[:].rearrange("p (j b t) -> p b j t", j=RH, b=CB)
                for r2 in range(2):
                    rows = slice(64 * r2, 64 * r2 + 64)
                    last = act.activation(qz[rows, c % 2, :, r2, :, :], q[rows], ACT.Copy, scale=HD ** -0.5)
                last.then_inc(q_ready, 1)

            def v_out(c, k):
                act.wait_ge(pe_vt, c * CG + k + 1)
                act.copy(vbd[:, c % 2, k * GB:(k + 1) * GB, :],
                         bank_kv[:].rearrange("p (b n) -> p b n", b=GB)).then_inc(v_ready, 1)

            def exp(c, k):
                act.wait_ge(shifted, c * CG + k + 1)
                v = sc[:, c % 2, k * GB:(k + 1) * GB, :]
                act.activation(v, v, ACT.Exp).then_inc(exp_ready, 1)

            def a_out(c, k):
                act.wait_ge(pe_pv, c * CG + k + 1)
                o = bank_sp[k][:].rearrange("p (b r j t) -> p r j b t", b=GB, r=2, j=RH)
                for r2 in range(2):
                    rows = slice(64 * r2, 64 * r2 + 64)
                    last = act.copy(aT[rows, c % 2, :, k * GB:(k + 1) * GB, :], o[rows, r2])
                last.then_inc(a_ready, 1)

            def z_out(c):
                act.wait_ge(pe_z, c + 1)
                act.copy(z_hi[:, c % 2], bank_yz[:].rearrange("p (f t) -> p f t", f=KT)).then_inc(zhi_ready, 1)

            def tanh(i):
                act.wait_ge(pe_gu, i + 1)
                act.activation(th[:, i % 2, :], bank_gu[i % 2][:, 0:CT], ACT.Tanh, scale=0.5).then_inc(tanh_ready, 1)

            def round_gated(i):
                act.wait_ge(gated_ready, i + 1)
                act.copy(g_hi[:, i % GRING, :], gated[:, i % GRING, :]).then_inc(ghi_ready, 1)

            for m in range(3):
                round_weights(m)
            q_out(0)
            v_out(0, 0)
            v_out(0, 1)
            round_weights(3)
            round_weights(4)
            exp(0, 0)
            exp(0, 1)
            round_weights(5)
            q_out(1)
            a_out(0, 0)
            a_out(0, 1)
            round_weights(6)
            round_weights(7)
            v_out(1, 0)
            z_out(0)
            v_out(1, 1)
            for c in range(NCH):
                for m in range(MT):
                    i = c * MT + m
                    if c + 1 < NCH:
                        if m in (0, 1) and c > 0:
                            v_out(c + 1, m)
                        if m in (2, 3):
                            exp(c + 1, m - 2)
                        if m == 6:
                            a_out(c + 1, 0)
                            a_out(c + 1, 1)
                    if c + 2 < NCH and m == 5:
                        q_out(c + 2)
                    tanh(i)
                    if i > 0:
                        round_gated(i - 1)
                    if c + 1 < NCH and m == MT - 1:
                        z_out(c + 1)
            round_gated(NCH * MT - 1)

        @block.vector
        def _(dve):
            def block_diagonal(c, src, dst, got, done):
                dve.wait_ge(got[c], 16 * CG)
                g = slice(c * CG, (c + 1) * CG)
                dve.tensor_tensor(dst[:, g], src[:, g].unsqueeze(2).to_broadcast([P, CG, GB, T]),
                                  batch_mask.unsqueeze(1).unsqueeze(3).to_broadcast([P, CG, GB, T]),
                                  ALU.mult).then_inc(done, 1)

            def side_rows(n):
                cols = BIAS_PARTS[n][0]
                b = slice(cols.start // T, cols.stop // T)
                shape = [NSUBJ, b.stop - b.start, T]
                dve.wait_ge(onehot_ready, 1)
                dve.wait_ge(ld_side, 16)
                dve.tensor_tensor(side_of[:, b], onehot[:, b].unsqueeze(2).to_broadcast(shape),
                                  side_sb[:].unsqueeze(1).to_broadcast(shape), ALU.mult).then_inc(side_ready, 1)

            def bias_out(n):
                cols, bnk = BIAS_PARTS[n]
                dve.wait_ge(pe_bias, n + 1)
                dve.tensor_copy(bias_bc[:, cols], bnk[:, 0:cols.stop - cols.start]).then_inc(bias_ready, 1)

            def y_out(c):
                dve.wait_ge(pe_y, c + 1)
                dve.wait_ge(bias_ready, min(c, 2) + 1)
                dve.tensor_tensor(yT[:, c % 2], bank_yz[:].rearrange("p (f t) -> p f t", f=KT),
                                  bias_bc[:, c * CT:(c + 1) * CT].unsqueeze(1).to_broadcast([P, KT, CT]),
                                  ALU.add).then_inc(y_ready, 1)

            def head_blocks(c, n, dst, done):
                dve.wait_ge(pe_kv, c + 1)
                src = bank_kv[:, n * CT:(n + 1) * CT].rearrange("p (b t) -> p b t", b=CB)
                dve.tensor_tensor(dst[:, c % 2], src.unsqueeze(2).to_broadcast([P, CB, KVH, T]),
                                  head_mask.unsqueeze(1).unsqueeze(3).to_broadcast([P, CB, KVH, T]),
                                  ALU.mult).then_inc(done, 1)

            def k_out(c):
                head_blocks(c, 0, kbd, kbd_ready)

            def v_blocks(c):
                head_blocks(c, 1, vbdT, vbdT_ready)

            def low_weights(m):
                dve.wait_ge(whi_ready, m + 1)
                dve.tensor_tensor(wf_lo[:, m, :], wf[:, m, :], wf_hi[:, m, :].bitcast(F32),
                                  ALU.subtract).then_inc(wlo_dve, 1)

            def row_max(c, k):
                n = c * CG + k
                v = sc[:, c % 2, k * GB:(k + 1) * GB, :]
                dve.wait_ge(pe_s, n + 1)
                dve.transpose(v.rearrange("p b n -> p (b n)"), bank_sp[k][:]).then_inc(s_turned, 1)
                dve.wait_ge(s_turned, n + 1)
                dve.tensor_tensor(v, v, alibi.unsqueeze(1).to_broadcast([P, GB, P]), ALU.add).then_inc(s_biased, 1)
                dve.wait_ge(s_biased, n + 1)
                dve.tensor_reduce(mx[:, c % 2, k * GB * REP:(k + 1) * GB * REP],
                                  v.rearrange("p b (r s) -> p (b r) s", s=T), AX_X, ALU.max).then_inc(max_ready, 1)

            def row_sum(c, k):
                n = c * CG + k
                cols = slice(k * GB * REP, (k + 1) * GB * REP)
                dve.wait_ge(exp_ready, n + 1)
                dve.tensor_reduce(sm[:, c % 2, cols],
                                  sc[:, c % 2, k * GB:(k + 1) * GB, :].rearrange("p b (r s) -> p (b r) s", s=T),
                                  AX_X, ALU.add).then_inc(sum_ready, 1)
                dve.wait_ge(sum_ready, n + 1)
                dve.reciprocal(rs[:, c % 2, cols], sm[:, c % 2, cols]).then_inc(recip_ready, 1)

            def turn_probs(c, k):
                dve.wait_ge(normed, c * CG + k + 1)
                b = slice(k * GB, (k + 1) * GB)
                dve.transpose(pT[:, c % 2, b, :].rearrange("p b n -> p (b n)"),
                              sc[:, c % 2, b, :].rearrange("p b n -> p (b n)")).then_inc(pT_ready, 1)

            def x1_out(c):
                g = slice(c * CG, (c + 1) * CG)
                dve.wait_ge(pe_wo, c + 1)
                dve.wait_ge(xb_ready, c + 1)
                dve.tensor_tensor(x1[:, g], bank_qo[:].rearrange("p (g f) -> p g f", g=CG), x1[:, g],
                                  ALU.add).then_inc(x1_ready, 1)

            def z_low(c):
                dve.wait_ge(zhi_ready, c + 1)
                dve.tensor_tensor(z_lo[:, c % 2], bank_yz[:].rearrange("p (f t) -> p f t", f=KT),
                                  z_hi[:, c % 2].bitcast(F32), ALU.subtract).then_inc(zlo_ready, 1)

            def gate(i):
                dve.wait_ge(tanh_ready, i + 1)
                dve.scalar_tensor_tensor(out=silu2[:, i % 2, :], in0=th[:, i % 2, :], scalar=1.0,
                                         in1=bank_gu[i % 2][:, 0:CT], op0=ALU.add, op1=ALU.mult).then_inc(silu_ready, 1)
                dve.wait_ge(silu_ready, i + 1)
                if i >= GRING:
                    dve.wait_ge(glo_ready, i - GRING + 1)
                dve.scalar_tensor_tensor(out=gated[:, i % GRING, :], in0=silu2[:, i % 2, :], scalar=0.5,
                                         in1=bank_gu[i % 2][:, CT:2 * CT], op0=ALU.mult,
                                         op1=ALU.mult).then_inc(gated_ready, 1)

            def result(c):
                g = slice(c * CG, (c + 1) * CG)
                dve.wait_ge(pe_dn, c + 1)
                if c >= 2:
                    dve.wait_ge(stored[c % 2], 16 * (c // 2))
                dve.tensor_tensor(out_sb[:, c % 2], bank_dn[:].rearrange("p (g f) -> p g f", g=CG), x1[:, g],
                                  ALU.add).then_inc(out_ready, 1)

            dve.memset(warm[:], 0.0).then_inc(warm_ready, 1)
            dve.memset(ones[:], 1.0).then_inc(ones_ready, 1)
            dve.wait_ge(ld_idx, 16)
            dve.scalar_tensor_tensor(out=idx[:], in0=idx_in[:, 0:2 * NG], scalar=float(T),
                                     in1=idx_in[:, 2 * NG:].to_broadcast([P, 2 * NG]), op0=ALU.mult,
                                     op1=ALU.add).then_inc(idx_ready, 1)
            dve.wait_ge(ld_subj, 16)
            dve.wait_ge(ld_tab, 16)
            dve.tensor_scalar(onehot[:], subj[:], number_of_p[0:NSUBJ], None, ALU.is_equal).then_inc(onehot_ready, 1)
            side_rows(0)
            block_diagonal(0, wc1, w1bd, got_w1, w1_ready)
            bias_out(0)
            side_rows(1)
            side_rows(2)
            y_out(0)
            low_weights(0)
            block_diagonal(1, wc1, w1bd, got_w1, w1_ready)
            k_out(0)
            v_blocks(0)
            bias_out(1)
            y_out(1)
            row_max(0, 0)
            row_max(0, 1)
            low_weights(1)
            row_sum(0, 0)
            row_sum(0, 1)
            turn_probs(0, 0)
            turn_probs(0, 1)
            k_out(1)
            v_blocks(1)
            block_diagonal(0, wc2, w2bd, got_w2, w2_ready)
            bias_out(2)
            row_max(1, 0)
            x1_out(0)
            low_weights(2)
            z_low(0)
            row_max(1, 1)
            for c in range(NCH):
                for m in range(MT):
                    if c + 1 < NCH:
                        if m in (0, 1) and c > 0:
                            row_max(c + 1, m)
                        if m in (2, 3):
                            row_sum(c + 1, m - 2)
                        if m in (4, 5):
                            turn_probs(c + 1, m - 4)
                        if m == 6:
                            block_diagonal(c + 1, wc2, w2bd, got_w2, w2_ready)
                        if m == 7:
                            x1_out(c + 1)
                    if c + 2 < NCH:
                        if m == 0:
                            block_diagonal(c + 2, wc1, w1bd, got_w1, w1_ready)
                        if m == 2:
                            y_out(c + 2)
                        if m == 4:
                            k_out(c + 2)
                        if m == 5:
                            v_blocks(c + 2)
                    if m == 3 and c > 0:
                        result(c - 1)
                    gate(c * MT + m)
                    if c + 1 < NCH and m == MT - 1:
                        z_low(c + 1)
            result(NCH - 1)

        @block.tensor
        def _(pe):
            def keep_warm(n):
                for _ in range(n):
                    pe.matmul(bank_dn[:], warm[:, 0:P], warm[:], start=True, stop=True)

            def bias_mm(n):
                cols, bnk = BIAS_PARTS[n]
                pe.wait_ge(side_ready, n + 1)
                pe.wait_ge(ones_ready, 1)
                pe.matmul(bnk[:, 0:cols.stop - cols.start], ones[:],
                          side_of[:].rearrange("n b d -> n (b d)")[:, cols], start=True, stop=True).then_inc(pe_bias, 1)

            def y_mm(c):
                pe.wait_ge(ld_x[min(c, 2)], 16)
                pe.wait_ge(w1_ready, c + 1)
                if c > 1:
                    pe.wait_ge(zlo_ready, c - 1)
                for k in range(CG):
                    for ft in range(KT):
                        last = pe.matmul(bank_yz[:, ft * CT + k * P:ft * CT + (k + 1) * P],
                                         x_sb[:, c * CG + k, ft * P:(ft + 1) * P],
                                         w1bd[:, c * CG + k].rearrange("p b d -> p (b d)"), start=True, stop=True)
                last.then_inc(pe_y, 1)

            def q_mm(c):
                pe.wait_ge(y_ready, c + 1)
                if c > 1:
                    pe.wait_ge(x1_ready, c - 1)
                for j in range(RH):
                    for ft in range(KT):
                        last = pe.matmul(bank_qo[:, j * CT:(j + 1) * CT], wqkv_sb[:, ft, j * P:(j + 1) * P],
                                         yT[:, c % 2, ft, :], start=(ft == 0), stop=(ft == KT - 1))
                last.then_inc(pe_q, 1)

            def kv_mm(c):
                pe.wait_ge(y_ready, c + 1)
                pe.wait_ge(ld_wqkv, 16)
                if c > 0:
                    pe.wait_ge(v_ready, c * CG)
                for n in range(2):
                    for ft in range(KT):
                        last = pe.matmul(bank_kv[:, n * CT:(n + 1) * CT],
                                         wqkv_sb[:, ft, C + n * P:C + (n + 1) * P],
                                         yT[:, c % 2, ft, :], start=(ft == 0), stop=(ft == KT - 1))
                last.then_inc(pe_kv, 1)

            def score_mm(c, k, bank_free, count):
                pe.wait_ge(q_ready, c + 1)
                pe.wait_ge(kbd_ready, c + 1)
                pe.wait_ge(bank_free, count)
                for b in range(GB):
                    last = pe.matmul(bank_sp[k][:, b * P:(b + 1) * P],
                                     kbd[:, c % 2, k * GB + b].rearrange("p g s -> p (g s)"),
                                     qz[:, c % 2, k * GB + b].rearrange("p r j t -> p (r j t)"),
                                     start=True, stop=True)
                last.then_inc(pe_s, 1)

            def turn_v(c, k):
                pe.wait_ge(vbdT_ready, c + 1)
                if k > 0:
                    pe.wait_ge(v_ready, c * CG + k)
                for b in range(GB):
                    last = pe.transpose(bank_kv[:, b * P:(b + 1) * P],
                                        vbdT[:, c % 2, k * GB + b].rearrange("p g s -> p (g s)"), ident)
                last.then_inc(pe_vt, 1)

            def pv_mm(c, k):
                pe.wait_ge(pT_ready, c * CG + k + 1)
                pe.wait_ge(v_ready, c * CG + k + 1)
                pe.wait_ge(s_turned, c * CG + k + 1)
                for b in range(GB):
                    last = pe.matmul(bank_sp[k][:, b * P:(b + 1) * P], vbd[:, c % 2, k * GB + b, :],
                                     pT[:, c % 2, k * GB + b, :], start=True, stop=True)
                last.then_inc(pe_pv, 1)

            def wo_mm(c):
                pe.wait_ge(a_ready, (c + 1) * CG)
                pe.wait_ge(ld_wo, 16)
                pe.wait_ge(q_ready, min(c + 2, NCH))
                for k in range(CG):
                    for j in range(RH):
                        last = pe.matmul(bank_qo[:, k * C:(k + 1) * C],
                                         aT[:, c % 2, j, k * GB:(k + 1) * GB, :].rearrange("p b t -> p (b t)"),
                                         wo_sb[:, j, :], start=(j == 0), stop=(j == RH - 1))
                last.then_inc(pe_wo, 1)

            def z_mm(c):
                pe.wait_ge(x1_ready, c + 1)
                pe.wait_ge(w2_ready, c + 1)
                for k in range(CG):
                    for ft in range(KT):
                        last = pe.matmul(bank_yz[:, ft * CT + k * P:ft * CT + (k + 1) * P],
                                         x1[:, c * CG + k, ft * P:(ft + 1) * P],
                                         w2bd[:, c * CG + k].rearrange("p b d -> p (b d)"), start=True, stop=True)
                last.then_inc(pe_z, 1)

            def up_mm(i):
                c, m = i // MT, i % MT
                pe.wait_ge(zlo_ready, c + 1)
                if m < DVE_LOW:
                    pe.wait_ge(wlo_dve, m + 1)
                else:
                    pe.wait_ge(wlo_pool, m + 1 - DVE_LOW)
                if i > 1:
                    pe.wait_ge(gated_ready, i - 1)
                else:
                    pe.wait_ge(bias_ready, i + 2)
                for n in range(2):
                    at = 0
                    for ft in range(KT):
                        cols = slice((n * KT + ft) * P, (n * KT + ft + 1) * P)
                        for w, z in ((wf_hi, z_hi), (wf_hi, z_lo), (wf_lo, z_hi)):
                            last = pe.matmul(bank_gu[i % 2][:, n * CT:(n + 1) * CT], w[:, m, cols],
                                             z[:, c % 2, ft, :], start=(at == 0), stop=(at == 3 * KT - 1))
                            at += 1
                last.then_inc(pe_gu, 1)

            def down_mm(i):
                c, m = i // MT, i % MT
                pe.wait_ge(glo_ready, i + 1)
                if m == 0 and c > 0:
                    pe.wait_ge(out_ready, c)
                for k in range(CG):
                    for n, (g, w) in enumerate(((g_hi, wf_hi), (g_hi, wf_lo), (g_lo, wf_hi))):
                        last = pe.matmul(bank_dn[:, k * C:(k + 1) * C], g[:, i % GRING, k * P:(k + 1) * P],
                                         w[:, m, 2 * C:3 * C], start=(m == 0 and k == 0 and n == 0),
                                         stop=(m == MT - 1 and n == 2), skip_group_check=True)
                if m == MT - 1:
                    last.then_inc(pe_dn, 1)

            pe.wait_ge(warm_ready, 1)
            keep_warm(WARM[0])
            pe.wait_ge(ld_tab, 16)
            bias_mm(0)
            keep_warm(WARM[1])
            y_mm(0)
            bias_mm(1)
            kv_mm(0)
            q_mm(0)
            y_mm(1)
            turn_v(0, 0)
            score_mm(0, 0, bias_ready, 1)
            score_mm(0, 1, bias_ready, 1)
            turn_v(0, 1)
            keep_warm(WARM[2])
            kv_mm(1)
            q_mm(1)
            bias_mm(2)
            keep_warm(WARM[3])
            pv_mm(0, 0)
            pv_mm(0, 1)
            score_mm(1, 0, a_ready, 1)
            wo_mm(0)
            score_mm(1, 1, a_ready, 2)
            turn_v(1, 0)
            keep_warm(WARM[4])
            z_mm(0)
            turn_v(1, 1)
            keep_warm(WARM[5])
            for i in range(NCH * MT + LAG):
                c, m = i // MT, i % MT
                if c + 1 < NCH:
                    if m in (0, 1) and c > 0:
                        score_mm(c + 1, m, a_ready, c * CG + m + 1)
                        turn_v(c + 1, m)
                    if m == 6:
                        pv_mm(c + 1, 0)
                        pv_mm(c + 1, 1)
                    if m == 7:
                        wo_mm(c + 1)
                if c + 2 < NCH:
                    if m == 2:
                        y_mm(c + 2)
                    if m == 3:
                        kv_mm(c + 2)
                    if m == 4:
                        q_mm(c + 2)
                if i >= LAG:
                    down_mm(i - LAG)
                if i < NCH * MT:
                    up_mm(i)
                if c + 1 < NCH and m == MT - 1:
                    z_mm(c + 1)


def kernel(**inputs):
    import concourse.bacc as bacc
    from concourse.bass_utils import run_bass_kernel_spmd

    def lay(a):
        return np.ascontiguousarray(a)

    a = {k: np.asarray(v) for k, v in inputs.items()}
    x = a["x"].reshape(B * T, C)
    index = [np.repeat(a[n].reshape(NG, GB).T, T, axis=0) for n in ("itok_B_0_7", "itok_B_1_198")]
    row_of_p = (np.arange(P) % T).astype(index[0].dtype)[:, None]
    wk, wv = a["L0_attn_Wkv"][:, :KVH * HD], a["L0_attn_Wkv"][:, KVH * HD:]
    w_qkv = np.concatenate([a["L0_attn_Wq"], wk, wk, wv, wv], axis=1).reshape(KT, P, 2 * C)
    gate_up = [a[n].reshape(MT, P, KT, P).transpose(3, 0, 2, 1).reshape(P, MT, C)
               for n in ("L0_ffn_w_gate", "L0_ffn_w_up")]
    down = a["L0_ffn_w_down"].reshape(C, MT, P).transpose(2, 1, 0)
    arrays = {
        "x": lay(x),
        "index": lay(np.concatenate(index + [row_of_p], axis=1)),
        "subject_row": lay(np.broadcast_to(a["itok_B_0_7"], (NSUBJ, B))),
        "side": lay(a["fside_8xS_0"]),
        "table": tables(),
        "w_cond": lay(a["L0_cond_weights"]),
        "w_cond2": lay(a["L0_cond2_weights"]),
        "w_qkv": lay(w_qkv.transpose(1, 0, 2)),
        "w_o": lay(a["L0_attn_Wo"].reshape(KT, P, C).transpose(1, 0, 2)),
        "b_o": lay(np.broadcast_to(a["L0_attn_bo"], (P, C))),
        "w_ffn": lay(np.concatenate(gate_up + [down], axis=2)),
    }
    nc = bacc.Bacc("TRN2", target_bir_lowering=False, num_devices=1)
    aps = [nc.dram_tensor(f"in_{k}", v.shape, mybir.dt.from_np(v.dtype), kind="ExternalInput").ap()
           for k, v in arrays.items()]
    out = nc.dram_tensor("out_x", (B * T, C), F32, kind="ExternalOutput").ap()
    adaln_attn_ffn(nc, *aps, out)
    r = run_bass_kernel_spmd(nc, [{f"in_{k}": v for k, v in arrays.items()}], core_ids=[0])
    return r.results[0]["out_x"].reshape(B, T, C)
```

```python
from contextlib import ExitStack

import numpy as np

import concourse.bass as bass
from concourse import mybir

F32 = mybir.dt.float32
F32R = mybir.dt.float32r
I32 = mybir.dt.int32
BF16 = mybir.dt.bfloat16
ALU = mybir.AluOpType
ACT = mybir.ActivationFunctionType
AX_X = mybir.AxisListType.X

P = 128
B, T, C = 32, 32, 256
H, KVH = 16, 4
HD = C // H
REP = H // KVH
NSUBJ, NCOND = 8, 200
HID = 1024
GB = P // T
NG = B // GB
CG = 2
NCH = NG // CG
CB = CG * GB
CT = CG * P
KT = C // P
RH = REP // 2
MT = HID // P
GRING = 6
DVE_TILES = (2, 4, 6)
POOL_TILES = (0, 1, 3, 5, 7)
PLAIN = 2
LAST = NCH * MT - 1
LAG = 4
MASKED = -1.0e38


def tables():
    p = np.arange(P)
    ident = np.eye(P, dtype=np.float32)
    start = 2.0 ** (-2.0 ** (-(np.log2(H) - 3.0)))
    slopes = np.array([start ** (i + 1) for i in range(H)], np.float32)
    g, t = (p // T)[:, None, None, None], (p % T)[:, None, None, None]
    r2, j, s = np.arange(2)[:, None, None], np.arange(RH)[:, None], np.arange(T)
    slope = slopes[(2 * j + r2) * KVH + g]
    alibi = np.where(s <= t, slope * (s - t).astype(np.float32), np.float32(MASKED))
    alibi = np.broadcast_to(alibi, (P, 2, RH, T)).reshape(P, P).astype(np.float32)
    head = (((p // HD) % KVH)[:, None] == np.arange(KVH)).astype(np.float32)
    batch = ((p // T)[:, None] == np.arange(GB)).astype(np.float32)
    number = p[:, None].astype(np.float32)
    return np.ascontiguousarray(np.concatenate([ident, alibi, head, batch, number], axis=1))


NTAB = 2 * P + KVH + GB + 1


def adaln_attn_ffn(nc, x, index, subject_row, side, table, w_cond, w_cond2, w_qkv, w_o, b_o, w_ffn, out):
    ctx = ExitStack()
    with ctx:
        def sb(name, shape, dt=F32):
            return ctx.enter_context(nc.sbuf_tensor(name, shape, dt))

        def bank(name):
            return ctx.enter_context(nc.psum_tensor(name, [P, 512], F32))

        def sem(name):
            return ctx.enter_context(nc.semaphore(name))

        tab = sb("tab", [P, NTAB])
        ident = tab[:, 0:P]
        alibi = tab[:, P:2 * P]
        head_mask = tab[:, 2 * P:2 * P + KVH]
        batch_mask = tab[:, 2 * P + KVH:2 * P + KVH + GB]
        number_of_p = tab[:, 2 * P + KVH + GB:NTAB]
        idx_in = sb("idx_in", [P, 2 * NG + 1], I32)
        idx = sb("idx", [P, 2 * NG], I32)
        subj = sb("subj", [NSUBJ, B], I32)
        side_sb = sb("side_sb", [NSUBJ, T])
        onehot = sb("onehot", [NSUBJ, B])
        side_of = sb("side_of", [NSUBJ, B, T])
        ones = sb("ones", [NSUBJ, P])
        bias_bc = sb("bias_bc", [P, B * T])
        wc1 = sb("wc1", [P, NG, T])
        wc2 = sb("wc2", [P, NG, T])
        w1bd = sb("w1bd", [P, NG, GB, T])
        w2bd = sb("w2bd", [P, NG, GB, T])
        wqkv_sb = sb("wqkv_sb", [P, KT, 2 * C])
        wqkv_hi = sb("wqkv_hi", [P, KT, 2 * C], F32R)
        wqkv_lo = sb("wqkv_lo", [P, KT, 2 * C], F32R)
        wo_sb = sb("wo_sb", [P, KT, C])
        wo_hi = sb("wo_hi", [P, KT, C], F32R)
        wo_lo = sb("wo_lo", [P, KT, C], F32R)
        bo_sb = sb("bo_sb", [P, C])
        wf = sb("wf", [P, MT, 3 * C])
        wf_hi = sb("wf_hi", [P, MT, 3 * C], F32R)
        wf_lo = sb("wf_lo", [P, MT, 3 * C], F32R)
        x_sb = sb("x_sb", [P, NG, C])
        x1 = sb("x1", [P, NG, C])
        yT = sb("yT", [P, 2, KT, CT])
        y_hi = sb("y_hi", [P, KT, CT], F32R)
        y_lo = sb("y_lo", [P, KT, CT], F32R)
        qz = sb("qz", [P, CB, 2, RH, T])
        kbd = sb("kbd", [P, CB, KVH, T])
        vbdT = sb("vbdT", [P, CB, KVH, T])
        vbd = sb("vbd", [P, 2, CB, P])
        sc = sb("sc", [P, 2, CB, P])
        mx = sb("mx", [P, 2, CB * REP])
        sm = sb("sm", [P, 2, CB * REP])
        rs = sb("rs", [P, 2, CB * REP])
        pT = sb("pT", [P, 2, CB, P])
        a_hi = sb("a_hi", [P, RH, CB, T], F32R)
        a_lo = sb("a_lo", [P, RH, CB, T], F32R)
        z_hi = sb("z_hi", [P, 2, KT, CT], F32R)
        z_lo = sb("z_lo", [P, 2, KT, CT], F32R)
        th = sb("th", [P, 2, CT])
        silu2 = sb("silu2", [P, 2, CT])
        gated = sb("gated", [P, GRING, CT])
        a_first = gated[:, 0:RH, :].rearrange("p j (b t) -> p j b t", b=CB)
        g_hi = sb("g_hi", [P, GRING, CT], F32R)
        g_lo = sb("g_lo", [P, GRING, CT], F32R)

        warm = sb("warm", [P, 512], BF16)

        bank_yz = bank("bank_yz")
        bank_qo = bank("bank_qo")
        bank_kv = bank("bank_kv")
        bank_sp = [bank("bank_sp0"), bank("bank_sp1")]
        bank_gu = [bank("bank_gu0"), bank("bank_gu1")]
        bank_dn = bank("bank_dn")

        ld_idx, ld_tab, ld_subj, ld_side = sem("ld_idx"), sem("ld_tab"), sem("ld_subj"), sem("ld_side")
        ld_x = [sem("ld_x0"), sem("ld_x1"), sem("ld_x23")]
        ld_wqkv = sem("ld_wqkv")
        ld_wo, ld_bo = sem("ld_wo"), sem("ld_bo")
        ld_wf = [sem(f"ld_wf{m}") for m in range(MT)]
        got_w1 = [sem(f"got_w1_{c}") for c in range(NCH)]
        got_w2 = [sem(f"got_w2_{c}") for c in range(NCH)]
        stored = sem("stored")
        pe_bias, pe_y, pe_q, pe_k, pe_v = sem("pe_bias"), sem("pe_y"), sem("pe_q"), sem("pe_k"), sem("pe_v")
        pe_s, pe_vt, pe_pv = sem("pe_s"), sem("pe_vt"), sem("pe_pv")
        pe_wo, pe_z, pe_gu, pe_dn = sem("pe_wo"), sem("pe_z"), sem("pe_gu"), sem("pe_dn")
        warm_ready, idx_ready, onehot_ready, side_ready = (
            sem("warm_ready"), sem("idx_ready"), sem("onehot_ready"), sem("side_ready"))
        ones_ready = sem("ones_ready")
        w1_ready, w2_ready, y_ready, ylo_ready = sem("w1_ready"), sem("w2_ready"), sem("y_ready"), sem("ylo_ready")
        wqkv_low, wo_low, alo_ready = sem("wqkv_low"), sem("wo_low"), sem("alo_ready")
        kbd_ready, vbdT_ready = sem("kbd_ready"), sem("vbdT_ready")
        s_turned, s_biased, max_ready = sem("s_turned"), sem("s_biased"), sem("max_ready")
        sum_ready, recip_ready, pT_ready = sem("sum_ready"), sem("recip_ready"), sem("pT_ready")
        x1_ready, zlo_ready, silu_ready, gated_ready = (
            sem("x1_ready"), sem("zlo_ready"), sem("silu_ready"), sem("gated_ready"))
        out_ready, wlo_dve = sem("out_ready"), sem("wlo_dve")
        bias_ready = sem("bias_ready")
        q_ready, v_ready, exp_ready, ahi_ready = sem("q_ready"), sem("v_ready"), sem("exp_ready"), sem("ahi_ready")
        yhi_ready, wqkv_high, wo_high = sem("yhi_ready"), sem("wqkv_high"), sem("wo_high")
        zhi_ready, tanh_ready, ghi_ready, whi_ready = (
            sem("zhi_ready"), sem("tanh_ready"), sem("ghi_ready"), sem("whi_ready"))
        qz_zeroed, xb_ready, shifted, normed = sem("qz_zeroed"), sem("xb_ready"), sem("shifted"), sem("normed")
        glo_ready, wlo_pool = sem("glo_ready"), sem("wlo_pool")

        BIAS_PARTS = [(slice(0, CT), bank_sp[0]), (slice(CT, 2 * CT), bank_sp[1]), (slice(2 * CT, 4 * CT), bank_dn)]
        FIRST_Q = [bank_qo, bank_gu[1]]
        FIRST_KV = [bank_kv, bank_gu[0]]
        FIRST_WO = [bank_dn, bank_gu[1]]
        FIRST_Z = [bank_yz, bank_gu[0]]

        def down_bank(c, k):
            return bank_yz[:, 0:C] if c == NCH - 1 and k == 1 else bank_dn[:, k * C:(k + 1) * C]

        def halves(c):
            return 2 + c

        def kv_bank(c, n):
            cols = FIRST_KV[n][:, 0:CT] if c == 0 else (bank_gu[0] if c == 1 else bank_kv)[:, n * CT:(n + 1) * CT]
            return cols.rearrange("p (b t) -> p b t", b=CB)

        x_rows = x.rearrange("(g p) f -> p g f", p=P)
        out_rows = out.rearrange("(g p) f -> p g f", p=P)

        block = ctx.enter_context(nc.Block())

        @block.sync
        def _(sp):
            sp.dma_start(idx_in[:], index).then_inc(ld_idx, 16)
            sp.dma_start(x_sb[:, 0:CG, :], x_rows[:, 0:CG, :]).then_inc(ld_x[0], 16)
            sp.dma_start(tab[:], table).then_inc(ld_tab, 16)
            sp.dma_start(subj[:], subject_row).then_inc(ld_subj, 16)
            sp.dma_start(side_sb[:], side).then_inc(ld_side, 16)
            sp.dma_start(wqkv_sb[:], w_qkv).then_inc(ld_wqkv, 16)
            sp.wait_ge(got_w1[0], 16 * CG)
            sp.dma_start(x_sb[:, CG:2 * CG, :], x_rows[:, CG:2 * CG, :]).then_inc(ld_x[1], 16)
            for m in range(MT):
                sp.dma_start(wf[:, m, :], w_ffn[:, m, :]).then_inc(ld_wf[m], 16)
                if m == 0:
                    sp.dma_start(bo_sb[:], b_o).then_inc(ld_bo, 16)
                if m == 2:
                    sp.dma_start(wo_sb[:], w_o).then_inc(ld_wo, 16)
                if m == 4:
                    sp.dma_start(x_sb[:, 2 * CG:NG, :], x_rows[:, 2 * CG:NG, :]).then_inc(ld_x[2], 16)
            for c in range(NCH - 1):
                sp.wait_ge(out_ready, c + 1)
                sp.dma_start(out_rows[:, c * CG:(c + 1) * CG, :], x1[:, c * CG:(c + 1) * CG, :]).then_inc(stored, 16)
            for k in range(CG):
                sp.wait_ge(out_ready, NCH + k)
                g = (NCH - 1) * CG + k
                sp.dma_start(out_rows[:, g, :], x1[:, g, :]).then_inc(stored, 16)
            sp.wait_ge(stored, 16 * (NCH - 1 + CG))

        @block.gpsimd
        def _(pool):
            def gather(table_rows, dst, col, grp, done):
                pool.indirect_dma_start(
                    dst[:, grp, :], None, table_rows,
                    bass.IndirectOffsetOnAxis(ap=idx[:, col + grp:col + grp + 1], axis=0)).then_inc(done, 16)

            def gather1(c):
                for grp in range(c * CG, (c + 1) * CG):
                    gather(w_cond.rearrange("n c d -> (n c) d"), wc1, 0, grp, got_w1[c])

            def gather2(c):
                for grp in range(c * CG, (c + 1) * CG):
                    gather(w_cond2.rearrange("n c d -> (n c) d"), wc2, NG, grp, got_w2[c])

            def add_bo(c):
                pool.wait_ge(ld_x[min(c, 2)], 16)
                pool.wait_ge(ld_bo, 16)
                pool.tensor_tensor(x1[:, c * CG:(c + 1) * CG, :], x_sb[:, c * CG:(c + 1) * CG, :],
                                   bo_sb[:].unsqueeze(1).to_broadcast([P, CG, C]), ALU.add).then_inc(xb_ready, 1)

            def shift(c, k):
                n = c * CG + k
                pool.wait_ge(max_ready, n + 1)
                v = sc[:, c % 2, k * GB:(k + 1) * GB, :].rearrange("p b (r s) -> p (b r) s", s=T)
                m = mx[:, c % 2, k * GB * REP:(k + 1) * GB * REP]
                pool.tensor_tensor(v, v, m.unsqueeze(2).to_broadcast([P, GB * REP, T]),
                                   ALU.subtract).then_inc(shifted, 1)

            def norm(c, k):
                n = c * CG + k
                pool.wait_ge(recip_ready, n + 1)
                v = sc[:, c % 2, k * GB:(k + 1) * GB, :].rearrange("p b (r s) -> p (b r) s", s=T)
                m = rs[:, c % 2, k * GB * REP:(k + 1) * GB * REP]
                pool.tensor_tensor(v, v, m.unsqueeze(2).to_broadcast([P, GB * REP, T]),
                                   ALU.mult).then_inc(normed, 1)

            def low_weights(m):
                pool.wait_ge(whi_ready, m + 1)
                pool.tensor_tensor(wf_lo[:, m, :], wf[:, m, :], wf_hi[:, m, :].bitcast(F32),
                                   ALU.subtract).then_inc(wlo_pool, 1)

            def low_gated(i):
                pool.wait_ge(ghi_ready, i + 1)
                pool.tensor_tensor(g_lo[:, i % GRING, :], gated[:, i % GRING, :],
                                   g_hi[:, i % GRING, :].bitcast(F32), ALU.subtract).then_inc(glo_ready, 1)

            def y_low(c):
                pool.wait_ge(yhi_ready, c + 1 - PLAIN)
                if c > PLAIN:
                    pool.wait_ge(pe_q, halves(c - 1))
                    pool.wait_ge(pe_v, c)
                pool.tensor_tensor(y_lo[:], yT[:, c % 2], y_hi[:].bitcast(F32), ALU.subtract).then_inc(ylo_ready, 1)

            def low_qkv():
                pool.wait_ge(wqkv_high, 1)
                pool.tensor_tensor(wqkv_lo[:], wqkv_sb[:], wqkv_hi[:].bitcast(F32), ALU.subtract).then_inc(wqkv_low, 1)

            def low_wo():
                pool.wait_ge(wo_high, 1)
                pool.tensor_tensor(wo_lo[:], wo_sb[:], wo_hi[:].bitcast(F32), ALU.subtract).then_inc(wo_low, 1)

            pool.memset(qz[:].rearrange("p b r j t -> p (b r j t)"), 0.0).then_inc(qz_zeroed, 1)
            pool.wait_ge(idx_ready, 1)
            gather1(0)
            gather1(1)
            gather2(0)
            add_bo(0)
            add_bo(1)
            low_weights(0)
            gather1(2)
            shift(0, 0)
            shift(0, 1)
            norm(0, 0)
            norm(0, 1)
            low_qkv()
            low_weights(1)
            gather2(1)
            low_weights(3)
            low_weights(5)
            shift(1, 0)
            y_low(2)
            shift(1, 1)
            low_gated(0)
            low_gated(1)
            norm(1, 0)
            low_gated(2)
            norm(1, 1)
            low_wo()
            low_gated(3)
            low_weights(7)
            low_gated(4)
            low_gated(5)
            gather1(3)
            low_gated(6)
            gather2(2)
            for c in range(1, NCH):
                for m in range(MT):
                    if c == 1 and m == 6: gather2(3)
                    if m == 4 and c + 1 < NCH: norm(c + 1, 1)
                    if m == 1 and c + 2 < NCH: y_low(c + 2)
                    if m == 0 and c + 1 < NCH: shift(c + 1, 0)
                    if m == 2 and c + 1 < NCH: norm(c + 1, 0)
                    if m == 5 and c + 1 < NCH: add_bo(c + 1)
                    if m >= 0: low_gated(c * MT + m - 1)
                    if m == 0 and c + 1 < NCH: shift(c + 1, 1)

        @block.scalar
        def _(act):
            def round_weights(m):
                act.wait_ge(ld_wf[m], 16)
                act.copy(wf_hi[:, m, :], wf[:, m, :]).then_inc(whi_ready, 1)

            def round_qkv():
                act.wait_ge(ld_wqkv, 16)
                act.copy(wqkv_hi[:], wqkv_sb[:]).then_inc(wqkv_high, 1)

            def round_wo():
                act.wait_ge(ld_wo, 16)
                act.copy(wo_hi[:], wo_sb[:]).then_inc(wo_high, 1)

            def bias_out(n):
                cols, bnk = BIAS_PARTS[n]
                act.wait_ge(pe_bias, n + 1)
                act.copy(bias_bc[:, cols], bnk[:, 0:cols.stop - cols.start]).then_inc(bias_ready, 1)

            def round_y(c):
                act.wait_ge(y_ready, c + 1)
                if c > PLAIN:
                    act.wait_ge(pe_q, halves(c - 1))
                    act.wait_ge(pe_v, c)
                act.copy(y_hi[:], yT[:, c % 2]).then_inc(yhi_ready, 1)

            def first_q_out(j):
                act.wait_ge(pe_q, j + 1)
                act.wait_ge(qz_zeroed, 1)
                for r2 in range(2):
                    rows = slice(64 * r2, 64 * r2 + 64)
                    last = act.activation(qz[rows, :, r2, j, :],
                                          FIRST_Q[j][rows, 0:CT].rearrange("p (b t) -> p b t", b=CB),
                                          ACT.Copy, scale=HD ** -0.5)
                if j == RH - 1:
                    last.then_inc(q_ready, 1)

            def q_out(c):
                act.wait_ge(pe_q, halves(c))
                act.wait_ge(pe_s, c * CG)
                q = bank_qo[:].rearrange("p (j b t) -> p b j t", j=RH, b=CB)
                for r2 in range(2):
                    rows = slice(64 * r2, 64 * r2 + 64)
                    last = act.activation(qz[rows, :, r2, :, :], q[rows], ACT.Copy, scale=HD ** -0.5)
                last.then_inc(q_ready, 1)

            def v_blocks(c):
                act.wait_ge(pe_v, c + 1)
                if c > 0:
                    act.wait_ge(kbd_ready, c + 1)
                    act.wait_ge(pe_vt, c * CG)
                for g in range(KVH):
                    last = act.activation(vbdT[:, :, g, :], kv_bank(c, 1), ACT.Copy, scale=head_mask[:, g:g + 1])
                last.then_inc(vbdT_ready, 1)

            def v_out(c, k):
                act.wait_ge(pe_vt, c * CG + k + 1)
                act.copy(vbd[:, c % 2, k * GB:(k + 1) * GB, :],
                         bank_kv[:].rearrange("p (b n) -> p b n", b=GB)).then_inc(v_ready, 1)

            def exp(c, k):
                act.wait_ge(shifted, c * CG + k + 1)
                v = sc[:, c % 2, k * GB:(k + 1) * GB, :]
                act.activation(v, v, ACT.Exp).then_inc(exp_ready, 1)

            def a_out(c, k):
                act.wait_ge(pe_pv, c * CG + k + 1)
                if c > 1:
                    act.wait_ge(pe_wo, halves(c - 1))
                dst = a_hi[:] if c > 0 else a_first
                o = bank_sp[k][:].rearrange("p (b r j t) -> p r j b t", b=GB, r=2, j=RH)
                for r2 in range(2):
                    rows = slice(64 * r2, 64 * r2 + 64)
                    last = act.copy(dst[rows, :, k * GB:(k + 1) * GB, :], o[rows, r2])
                last.then_inc(ahi_ready, 1)

            def first_z_out(k):
                act.wait_ge(pe_z, k + 1)
                act.copy(z_hi[:, 0, :, k * P:(k + 1) * P],
                         FIRST_Z[k][:, 0:KT * P].rearrange("p (f t) -> p f t", f=KT)).then_inc(zhi_ready, 1)

            def z_out(c):
                act.wait_ge(pe_z, halves(c))
                act.copy(z_hi[:, c % 2], bank_yz[:].rearrange("p (f t) -> p f t", f=KT)).then_inc(zhi_ready, 1)

            def tanh(i):
                act.wait_ge(pe_gu, i + 1)
                act.activation(th[:, i % 2, :], bank_gu[i % 2][:, 0:CT], ACT.Tanh, scale=0.5).then_inc(tanh_ready, 1)

            def round_gated(i):
                act.wait_ge(gated_ready, i + 1)
                act.copy(g_hi[:, i % GRING, :], gated[:, i % GRING, :]).then_inc(ghi_ready, 1)

            bias_out(0)
            round_qkv()
            first_q_out(0)
            round_weights(0)
            bias_out(1)
            first_q_out(1)
            v_blocks(0)
            round_weights(1)
            v_out(0, 0)
            round_weights(2)
            exp(0, 0)
            exp(0, 1)
            v_out(0, 1)
            q_out(1)
            bias_out(2)
            a_out(0, 0)
            a_out(0, 1)
            v_blocks(1)
            first_z_out(0)
            first_z_out(1)
            round_weights(3)
            round_weights(4)
            round_weights(5)
            round_weights(6)
            v_out(1, 0)
            tanh(0)
            round_y(2)
            v_out(1, 1)
            exp(1, 0)
            tanh(1)
            round_gated(0)
            tanh(2)
            round_gated(1)
            round_weights(7)
            exp(1, 1)
            round_wo()
            tanh(3)
            round_gated(2)
            tanh(4)
            tanh(5)
            q_out(2)
            round_gated(3)
            a_out(1, 0)
            a_out(1, 1)
            round_gated(4)
            v_blocks(2)
            tanh(6)
            round_gated(5)
            tanh(7)
            z_out(1)
            round_gated(6)
            for c in range(1, NCH):
                for m in range(MT):
                    if m == 6 and c + 1 < NCH: a_out(c + 1, 1)
                    if m == 7 and c + 1 < NCH: z_out(c + 1)
                    if m == 5 and c + 2 < NCH: q_out(c + 2)
                    if m == 3 and c + 1 < NCH: exp(c + 1, 1)
                    if m == 5 and c + 1 < NCH: a_out(c + 1, 0)
                    if m == 2 and c + 1 < NCH: exp(c + 1, 0)
                    if m >= 0: tanh(c * MT + m)
                    if m == 0 and c + 1 < NCH: v_out(c + 1, 0)
                    if m >= 0: round_gated(c * MT + m - 1)
                    if m == 1 and c + 2 < NCH: round_y(c + 2)
                    if m == 6 and c + 2 < NCH: v_blocks(c + 2)
                    if m == 2 and c + 1 < NCH: v_out(c + 1, 1)

        @block.vector
        def _(dve):
            def block_diagonal(c, src, dst, got, done):
                dve.wait_ge(got[c], 16 * CG)
                g = slice(c * CG, (c + 1) * CG)
                dve.tensor_tensor(dst[:, g], src[:, g].unsqueeze(2).to_broadcast([P, CG, GB, T]),
                                  batch_mask.unsqueeze(1).unsqueeze(3).to_broadcast([P, CG, GB, T]),
                                  ALU.mult).then_inc(done, 1)

            def side_rows(n):
                cols = BIAS_PARTS[n][0]
                b = slice(cols.start // T, cols.stop // T)
                shape = [NSUBJ, b.stop - b.start, T]
                dve.wait_ge(onehot_ready, 1)
                dve.wait_ge(ld_side, 16)
                dve.tensor_tensor(side_of[:, b], onehot[:, b].unsqueeze(2).to_broadcast(shape),
                                  side_sb[:].unsqueeze(1).to_broadcast(shape), ALU.mult).then_inc(side_ready, 1)

            def y_out(c):
                dve.wait_ge(pe_y, c + 1)
                dve.wait_ge(bias_ready, min(c, 2) + 1)
                if c >= PLAIN:
                    dve.wait_ge(pe_q, halves(c - 2))
                    dve.wait_ge(pe_v, c - 1)
                dve.tensor_tensor(yT[:, c % 2], bank_yz[:].rearrange("p (f t) -> p f t", f=KT),
                                  bias_bc[:, c * CT:(c + 1) * CT].unsqueeze(1).to_broadcast([P, KT, CT]),
                                  ALU.add).then_inc(y_ready, 1)

            def a_low(c, k):
                dve.wait_ge(ahi_ready, c * CG + k + 1)
                if c > 1:
                    dve.wait_ge(pe_wo, halves(c - 1))
                o = bank_sp[k][:].rearrange("p (b r j t) -> p r j b t", b=GB, r=2, j=RH)
                for r2 in range(2):
                    rows = slice(64 * r2, 64 * r2 + 64)
                    cols = slice(k * GB, (k + 1) * GB)
                    last = dve.tensor_tensor(a_lo[rows, :, cols, :], o[rows, r2], a_hi[rows, :, cols, :].bitcast(F32),
                                             ALU.subtract)
                last.then_inc(alo_ready, 1)

            def k_out(c):
                dve.wait_ge(pe_k if c == 0 else pe_v, c + 1)
                if c > 0:
                    dve.wait_ge(pe_s, c * CG)
                dve.tensor_tensor(kbd[:], kv_bank(c, 0).unsqueeze(2).to_broadcast([P, CB, KVH, T]),
                                  head_mask.unsqueeze(1).unsqueeze(3).to_broadcast([P, CB, KVH, T]),
                                  ALU.mult).then_inc(kbd_ready, 1)

            def low_weights(m):
                dve.wait_ge(whi_ready, m + 1)
                dve.tensor_tensor(wf_lo[:, m, :], wf[:, m, :], wf_hi[:, m, :].bitcast(F32),
                                  ALU.subtract).then_inc(wlo_dve, 1)

            def row_max(c, k):
                n = c * CG + k
                v = sc[:, c % 2, k * GB:(k + 1) * GB, :]
                dve.wait_ge(pe_s, n + 1)
                dve.transpose(v.rearrange("p b n -> p (b n)"), bank_sp[k][:]).then_inc(s_turned, 1)
                dve.wait_ge(s_turned, n + 1)
                dve.tensor_tensor(v, v, alibi.unsqueeze(1).to_broadcast([P, GB, P]), ALU.add).then_inc(s_biased, 1)
                dve.wait_ge(s_biased, n + 1)
                dve.tensor_reduce(mx[:, c % 2, k * GB * REP:(k + 1) * GB * REP],
                                  v.rearrange("p b (r s) -> p (b r) s", s=T), AX_X, ALU.max).then_inc(max_ready, 1)

            def row_sum(c, k):
                n = c * CG + k
                cols = slice(k * GB * REP, (k + 1) * GB * REP)
                dve.wait_ge(exp_ready, n + 1)
                dve.tensor_reduce(sm[:, c % 2, cols],
                                  sc[:, c % 2, k * GB:(k + 1) * GB, :].rearrange("p b (r s) -> p (b r) s", s=T),
                                  AX_X, ALU.add).then_inc(sum_ready, 1)
                dve.wait_ge(sum_ready, n + 1)
                dve.reciprocal(rs[:, c % 2, cols], sm[:, c % 2, cols]).then_inc(recip_ready, 1)

            def turn_probs(c, k):
                dve.wait_ge(normed, c * CG + k + 1)
                b = slice(k * GB, (k + 1) * GB)
                dve.transpose(pT[:, c % 2, b, :].rearrange("p b n -> p (b n)"),
                              sc[:, c % 2, b, :].rearrange("p b n -> p (b n)")).then_inc(pT_ready, 1)

            def first_x1_out(k):
                dve.wait_ge(pe_wo, k + 1)
                dve.wait_ge(xb_ready, 1)
                dve.tensor_tensor(x1[:, k], FIRST_WO[k][:, 0:C], x1[:, k], ALU.add).then_inc(x1_ready, 1)

            def x1_out(c):
                g = slice(c * CG, (c + 1) * CG)
                dve.wait_ge(pe_wo, halves(c))
                dve.wait_ge(xb_ready, c + 1)
                dve.tensor_tensor(x1[:, g], bank_qo[:].rearrange("p (g f) -> p g f", g=CG), x1[:, g],
                                  ALU.add).then_inc(x1_ready, 1)

            def first_z_low(k):
                dve.wait_ge(zhi_ready, k + 1)
                cols = slice(k * P, (k + 1) * P)
                dve.tensor_tensor(z_lo[:, 0, :, cols], FIRST_Z[k][:, 0:KT * P].rearrange("p (f t) -> p f t", f=KT),
                                  z_hi[:, 0, :, cols].bitcast(F32), ALU.subtract).then_inc(zlo_ready, 1)

            def z_low(c):
                dve.wait_ge(zhi_ready, halves(c))
                dve.tensor_tensor(z_lo[:, c % 2], bank_yz[:].rearrange("p (f t) -> p f t", f=KT),
                                  z_hi[:, c % 2].bitcast(F32), ALU.subtract).then_inc(zlo_ready, 1)

            def gate(i):
                dve.wait_ge(tanh_ready, i + 1)
                dve.scalar_tensor_tensor(out=silu2[:, i % 2, :], in0=th[:, i % 2, :], scalar=1.0,
                                         in1=bank_gu[i % 2][:, 0:CT], op0=ALU.add, op1=ALU.mult).then_inc(silu_ready, 1)
                dve.wait_ge(silu_ready, i + 1)
                if i >= GRING:
                    dve.wait_ge(glo_ready, i - GRING + 1)
                dve.scalar_tensor_tensor(out=gated[:, i % GRING, :], in0=silu2[:, i % 2, :], scalar=0.5,
                                         in1=bank_gu[i % 2][:, CT:2 * CT], op0=ALU.mult,
                                         op1=ALU.mult).then_inc(gated_ready, 1)

            def result(c):
                g = slice(c * CG, (c + 1) * CG)
                dve.wait_ge(pe_dn, c + 1)
                dve.tensor_tensor(x1[:, g], bank_dn[:].rearrange("p (g f) -> p g f", g=CG), x1[:, g],
                                  ALU.add).then_inc(out_ready, 1)

            def last_result(k):
                dve.wait_ge(pe_dn, NCH + k)
                g = (NCH - 1) * CG + k
                dve.tensor_tensor(x1[:, g], down_bank(NCH - 1, k), x1[:, g], ALU.add).then_inc(out_ready, 1)

            dve.memset(warm[:], 0.0).then_inc(warm_ready, 1)
            dve.memset(ones[:], 1.0).then_inc(ones_ready, 1)
            dve.wait_ge(ld_idx, 16)
            dve.scalar_tensor_tensor(out=idx[:], in0=idx_in[:, 0:2 * NG], scalar=float(T),
                                     in1=idx_in[:, 2 * NG:].to_broadcast([P, 2 * NG]), op0=ALU.mult,
                                     op1=ALU.add).then_inc(idx_ready, 1)
            dve.wait_ge(ld_subj, 16)
            dve.wait_ge(ld_tab, 16)
            dve.tensor_scalar(onehot[:], subj[:], number_of_p[0:NSUBJ], None, ALU.is_equal).then_inc(onehot_ready, 1)
            side_rows(0)
            side_rows(1)
            block_diagonal(0, wc1, w1bd, got_w1, w1_ready)
            y_out(0)
            side_rows(2)
            block_diagonal(1, wc1, w1bd, got_w1, w1_ready)
            k_out(0)
            block_diagonal(0, wc2, w2bd, got_w2, w2_ready)
            y_out(1)
            row_max(0, 0)
            row_max(0, 1)
            row_sum(0, 0)
            row_sum(0, 1)
            turn_probs(0, 0)
            turn_probs(0, 1)
            k_out(1)
            block_diagonal(2, wc1, w1bd, got_w1, w1_ready)
            first_x1_out(0)
            first_x1_out(1)
            first_z_low(0)
            first_z_low(1)
            row_max(1, 0)
            low_weights(2)
            low_weights(4)
            y_out(2)
            gate(0)
            row_max(1, 1)
            gate(1)
            row_sum(1, 0)
            low_weights(6)
            gate(2)
            turn_probs(1, 0)
            block_diagonal(1, wc2, w2bd, got_w2, w2_ready)
            gate(3)
            row_sum(1, 1)
            k_out(2)
            turn_probs(1, 1)
            gate(4)
            gate(5)
            a_low(1, 0)
            a_low(1, 1)
            gate(6)
            x1_out(1)
            z_low(1)
            gate(7)
            for c in range(1, NCH):
                for m in range(MT):
                    if m == 5 and c + 1 < NCH: block_diagonal(c + 1, wc2, w2bd, got_w2, w2_ready)
                    if m == 0 and c + 1 < NCH: row_max(c + 1, 0)
                    if m == 2 and c + 1 < NCH: row_sum(c + 1, 0)
                    if m == 4 and c + 1 < NCH: row_sum(c + 1, 1)
                    if m == 3 and c + 1 < NCH: turn_probs(c + 1, 0)
                    if m == 1 and c + 1 < NCH: row_max(c + 1, 1)
                    if m == 6 and c + 1 < NCH: a_low(c + 1, 0)
                    if m == 6 and c + 1 < NCH: a_low(c + 1, 1)
                    if m == 7 and c + 1 < NCH: x1_out(c + 1)
                    if m == 5 and c + 2 < NCH: k_out(c + 2)
                    if m == 4 and c + 1 < NCH: turn_probs(c + 1, 1)
                    if m == 3 and c > 0: result(c - 1)
                    if m == 1 and c + 2 < NCH: y_out(c + 2)
                    if m == 0 and c + 2 < NCH: block_diagonal(c + 2, wc1, w1bd, got_w1, w1_ready)
                    if m == 7 and c + 1 < NCH: z_low(c + 1)
                    if m >= 0: gate(c * MT + m)
            for k in range(CG):
                last_result(k)

        @block.tensor
        def _(pe):
            def keep_warm(n, bnk):
                for _ in range(n):
                    pe.matmul(bnk[:], warm[:, 0:P], warm[:], start=True, stop=True)

            def bias_mm(n):
                cols, bnk = BIAS_PARTS[n]
                pe.wait_ge(side_ready, n + 1)
                pe.wait_ge(ones_ready, 1)
                pe.matmul(bnk[:, 0:cols.stop - cols.start], ones[:],
                          side_of[:].rearrange("n b d -> n (b d)")[:, cols], start=True, stop=True).then_inc(pe_bias, 1)

            def y_mm(c):
                pe.wait_ge(ld_x[min(c, 2)], 16)
                pe.wait_ge(w1_ready, c + 1)
                if c == 1:
                    pe.wait_ge(y_ready, 1)
                if c > 1:
                    pe.wait_ge(zlo_ready, halves(c - 2))
                for k in range(CG):
                    for ft in range(KT):
                        last = pe.matmul(bank_yz[:, ft * CT + k * P:ft * CT + (k + 1) * P],
                                         x_sb[:, c * CG + k, ft * P:(ft + 1) * P],
                                         w1bd[:, c * CG + k].rearrange("p b d -> p (b d)"), start=True, stop=True)
                last.then_inc(pe_y, 1)

            def three_passes(dst, lhs, rhs):
                for n, (l_hi, l_lo, r_hi, r_lo) in enumerate([(*a, *b) for a, b in zip(lhs, rhs)]):
                    pe.matmul(dst, l_hi, r_hi, start=(n == 0), stop=False)
                    pe.matmul(dst, l_hi, r_lo, start=False, stop=False)
                    last = pe.matmul(dst, l_lo, r_hi, start=False, stop=(n == len(lhs) - 1))
                return last

            def project_y(c, dst, col):
                cols = slice(col, col + P)
                return three_passes(dst, [(wqkv_hi[:, ft, cols], wqkv_lo[:, ft, cols]) for ft in range(KT)],
                                    [(y_hi[:, ft, :], y_lo[:, ft, :]) for ft in range(KT)])

            def plain_y(c, dst, col):
                for ft in range(KT):
                    last = pe.matmul(dst, wqkv_sb[:, ft, col:col + P], yT[:, c % 2, ft, :],
                                     start=(ft == 0), stop=(ft == KT - 1))
                return last

            def first_mm(dst, col, done):
                pe.wait_ge(y_ready, 1)
                pe.wait_ge(ld_wqkv, 16)
                plain_y(0, dst[:, 0:CT], col).then_inc(done, 1)

            def wait_y(c):
                if c < PLAIN:
                    pe.wait_ge(y_ready, c + 1)
                else:
                    pe.wait_ge(ylo_ready, c + 1 - PLAIN)
                    pe.wait_ge(wqkv_low, 1)

            def q_mm(c):
                wait_y(c)
                if c > 1:
                    pe.wait_ge(x1_ready, halves(c - 2))
                pe.wait_ge(q_ready, c)
                for j in range(RH):
                    last = (plain_y if c < PLAIN else project_y)(c, bank_qo[:, j * CT:(j + 1) * CT], j * P)
                last.then_inc(pe_q, 1)

            def kv_mm(c):
                wait_y(c)
                if c > 1:
                    pe.wait_ge(v_ready, c * CG)
                else:
                    pe.wait_ge(vbdT_ready, 1)
                for n, done in enumerate((pe_k, pe_v)):
                    (plain_y if c < PLAIN else project_y)(
                        c, kv_bank(c, n).rearrange("p b t -> p (b t)"), C + n * P).then_inc(done, 1)

            def score_mm(c, k, bank_free, count):
                pe.wait_ge(q_ready, c + 1)
                pe.wait_ge(kbd_ready, c + 1)
                pe.wait_ge(bank_free, count)
                for b in range(GB):
                    last = pe.matmul(bank_sp[k][:, b * P:(b + 1) * P],
                                     kbd[:, k * GB + b].rearrange("p g s -> p (g s)"),
                                     qz[:, k * GB + b].rearrange("p r j t -> p (r j t)"),
                                     start=True, stop=True)
                last.then_inc(pe_s, 1)

            def turn_v(c, k):
                pe.wait_ge(vbdT_ready, c + 1)
                if c * CG + k > 0:
                    pe.wait_ge(v_ready, c * CG + k)
                else:
                    pe.wait_ge(kbd_ready, 1)
                for b in range(GB):
                    last = pe.transpose(bank_kv[:, b * P:(b + 1) * P],
                                        vbdT[:, k * GB + b].rearrange("p g s -> p (g s)"), ident)
                last.then_inc(pe_vt, 1)

            def pv_mm(c, k):
                pe.wait_ge(pT_ready, c * CG + k + 1)
                pe.wait_ge(v_ready, c * CG + k + 1)
                pe.wait_ge(s_turned, c * CG + k + 1)
                for b in range(GB):
                    last = pe.matmul(bank_sp[k][:, b * P:(b + 1) * P], vbd[:, c % 2, k * GB + b, :],
                                     pT[:, c % 2, k * GB + b, :], start=True, stop=True)
                last.then_inc(pe_pv, 1)

            def first_wo_mm(k):
                pe.wait_ge(ahi_ready, k + 1)
                pe.wait_ge(ld_wo, 16)
                if k == 0:
                    pe.wait_ge(bias_ready, 3)
                for j in range(RH):
                    last = pe.matmul(FIRST_WO[k][:, 0:C],
                                     a_first[:, j, k * GB:(k + 1) * GB, :].rearrange("p b t -> p (b t)"),
                                     wo_sb[:, j, :], start=(j == 0), stop=(j == RH - 1))
                last.then_inc(pe_wo, 1)

            def wo_mm(c):
                pe.wait_ge(alo_ready, c * CG)
                pe.wait_ge(wo_low, 1)
                pe.wait_ge(q_ready, min(c + 2, NCH))
                for k in range(CG):
                    a = [tuple(x[:, j, k * GB:(k + 1) * GB, :].rearrange("p b t -> p (b t)") for x in (a_hi, a_lo))
                         for j in range(RH)]
                    last = three_passes(bank_qo[:, k * C:(k + 1) * C], a,
                                        [(wo_hi[:, j, :], wo_lo[:, j, :]) for j in range(RH)])
                last.then_inc(pe_wo, 1)

            def z_group(c, k, dst):
                for ft in range(KT):
                    last = pe.matmul(dst(ft), x1[:, c * CG + k, ft * P:(ft + 1) * P],
                                     w2bd[:, c * CG + k].rearrange("p b d -> p (b d)"), start=True, stop=True)
                return last

            def first_z_mm(k):
                pe.wait_ge(x1_ready, k + 1)
                pe.wait_ge(w2_ready, 1)
                if k == 0:
                    pe.wait_ge(y_ready, 2)
                else:
                    pe.wait_ge(vbdT_ready, 2)
                    pe.wait_ge(kbd_ready, 2)
                z_group(0, k, lambda ft: FIRST_Z[k][:, ft * P:(ft + 1) * P]).then_inc(pe_z, 1)

            def z_mm(c):
                pe.wait_ge(x1_ready, halves(c))
                pe.wait_ge(w2_ready, c + 1)
                pe.wait_ge(y_ready, min(c + 2, NCH))
                for k in range(CG):
                    last = z_group(c, k, lambda ft: bank_yz[:, ft * CT + k * P:ft * CT + (k + 1) * P])
                last.then_inc(pe_z, 1)

            def up_mm(i):
                c, m = i // MT, i % MT
                pe.wait_ge(zlo_ready, halves(c))
                if m in DVE_TILES:
                    pe.wait_ge(wlo_dve, DVE_TILES.index(m) + 1)
                else:
                    pe.wait_ge(wlo_pool, POOL_TILES.index(m) + 1)
                if i > 1:
                    pe.wait_ge(gated_ready, i - 1)
                for n in range(2):
                    cols = [slice((n * KT + ft) * P, (n * KT + ft + 1) * P) for ft in range(KT)]
                    last = three_passes(bank_gu[i % 2][:, n * CT:(n + 1) * CT],
                                        [(wf_hi[:, m, x], wf_lo[:, m, x]) for x in cols],
                                        [(z_hi[:, c % 2, ft, :], z_lo[:, c % 2, ft, :]) for ft in range(KT)])
                last.then_inc(pe_gu, 1)

            def down_mm(i):
                c, m = i // MT, i % MT
                if m == 0 and c > 0:
                    pe.wait_ge(out_ready, c)
                if i == LAST:
                    pe.wait_ge(gated_ready, i + 1)
                    parts = ((gated, wf),)
                else:
                    pe.wait_ge(glo_ready, i + 1)
                    parts = ((g_hi, wf_hi), (g_hi, wf_lo), (g_lo, wf_hi))
                for k in range(CG):
                    for n, (g, w) in enumerate(parts):
                        last = pe.matmul(down_bank(c, k), g[:, i % GRING, k * P:(k + 1) * P],
                                         w[:, m, 2 * C:3 * C],
                                         start=(m == 0 and n == 0 and (k == 0 or c == NCH - 1)),
                                         stop=(m == MT - 1 and n == len(parts) - 1), skip_group_check=True)
                    if i == LAST and k == 0:
                        last.then_inc(pe_dn, 1)
                if m == MT - 1:
                    last.then_inc(pe_dn, 1)

            pe.wait_ge(warm_ready, 1)
            keep_warm(12, bank_dn)
            bias_mm(0)
            bias_mm(1)
            y_mm(0)
            keep_warm(3, bank_dn)
            first_mm(FIRST_KV[0], C, pe_k)
            first_mm(FIRST_Q[0], 0, pe_q)
            first_mm(FIRST_Q[1], P, pe_q)
            first_mm(FIRST_KV[1], C + P, pe_v)
            y_mm(1)
            score_mm(0, 0, bias_ready, 1)
            score_mm(0, 1, bias_ready, 2)
            kv_mm(1)
            turn_v(0, 0)
            keep_warm(4, bank_dn)
            keep_warm(1, bank_dn)
            keep_warm(3, bank_dn)
            keep_warm(1, bank_dn)
            turn_v(0, 1)
            q_mm(1)
            bias_mm(2)
            pv_mm(0, 0)
            pv_mm(0, 1)
            first_wo_mm(0)
            first_wo_mm(1)
            first_z_mm(0)
            keep_warm(1, bank_dn)
            first_z_mm(1)
            score_mm(1, 0, ahi_ready, 1)
            turn_v(1, 0)
            up_mm(0)
            up_mm(1)
            y_mm(2)
            keep_warm(1, bank_dn)
            score_mm(1, 1, ahi_ready, 2)
            keep_warm(1, bank_dn)
            turn_v(1, 1)
            up_mm(2)
            kv_mm(2)
            q_mm(2)
            down_mm(0)
            up_mm(3)
            up_mm(4)
            down_mm(1)
            up_mm(5)
            pv_mm(1, 0)
            pv_mm(1, 1)
            down_mm(2)
            up_mm(6)
            wo_mm(1)
            down_mm(3)
            up_mm(7)
            z_mm(1)
            for i in range(MT, NCH * MT + LAG):
                c, m = i // MT, i % MT
                if m == 6 and c + 1 < NCH: pv_mm(c + 1, 1)
                if m == 3 and c + 1 < NCH: turn_v(c + 1, 1)
                if m == 5 and c + 1 < NCH: pv_mm(c + 1, 0)
                if m == 4 and c + 2 < NCH: q_mm(c + 2)
                if m == 0 and c + 1 < NCH: score_mm(c + 1, 0, alo_ready, (c - 1) * CG + 1)
                if m == 0 and c + 1 < NCH: turn_v(c + 1, 0)
                if m == 0 and c + 1 < NCH: score_mm(c + 1, 1, alo_ready, (c - 1) * CG + 2)
                if c < NCH: up_mm(i)
                if m == 1 and c + 2 < NCH: y_mm(c + 2)
                if m == 5 and c + 2 < NCH: kv_mm(c + 2)
                if m == 7 and c + 1 < NCH: wo_mm(c + 1)
                if i >= MT: down_mm(i - LAG)
                if m == 7 and c + 1 < NCH: z_mm(c + 1)


def kernel(**inputs):
    import concourse.bacc as bacc
    from concourse.bass_utils import run_bass_kernel_spmd

    def lay(a):
        return np.ascontiguousarray(a)

    a = {k: np.asarray(v) for k, v in inputs.items()}
    x = a["x"].reshape(B * T, C)
    index = [np.repeat(a[n].reshape(NG, GB).T, T, axis=0) for n in ("itok_B_0_7", "itok_B_1_198")]
    row_of_p = (np.arange(P) % T).astype(index[0].dtype)[:, None]
    wk, wv = a["L0_attn_Wkv"][:, :KVH * HD], a["L0_attn_Wkv"][:, KVH * HD:]
    w_qkv = np.concatenate([a["L0_attn_Wq"], wk, wk, wv, wv], axis=1).reshape(KT, P, 2 * C)
    gate_up = [a[n].reshape(MT, P, KT, P).transpose(3, 0, 2, 1).reshape(P, MT, C)
               for n in ("L0_ffn_w_gate", "L0_ffn_w_up")]
    down = a["L0_ffn_w_down"].reshape(C, MT, P).transpose(2, 1, 0)
    arrays = {
        "x": lay(x),
        "index": lay(np.concatenate(index + [row_of_p], axis=1)),
        "subject_row": lay(np.broadcast_to(a["itok_B_0_7"], (NSUBJ, B))),
        "side": lay(a["fside_8xS_0"]),
        "table": tables(),
        "w_cond": lay(a["L0_cond_weights"]),
        "w_cond2": lay(a["L0_cond2_weights"]),
        "w_qkv": lay(w_qkv.transpose(1, 0, 2)),
        "w_o": lay(a["L0_attn_Wo"].reshape(KT, P, C).transpose(1, 0, 2)),
        "b_o": lay(np.broadcast_to(a["L0_attn_bo"], (P, C))),
        "w_ffn": lay(np.concatenate(gate_up + [down], axis=2)),
    }
    nc = bacc.Bacc("TRN2", target_bir_lowering=False, num_devices=1)
    aps = [nc.dram_tensor(f"in_{k}", v.shape, mybir.dt.from_np(v.dtype), kind="ExternalInput").ap()
           for k, v in arrays.items()]
    out = nc.dram_tensor("out_x", (B * T, C), F32, kind="ExternalOutput").ap()
    adaln_attn_ffn(nc, *aps, out)
    r = run_bass_kernel_spmd(nc, [{f"in_{k}": v for k, v in arrays.items()}], core_ids=[0])
    return r.results[0]["out_x"].reshape(B, T, C)
```
